# Optimizing a Trainium2 kernel written in Bass

```python
import numpy as np
import jax
import jax.numpy as jnp

def _softmax(x, axis=-1):
    return jax.nn.softmax(x, axis=axis)

def _gelu(x):
    return jax.nn.gelu(x, approximate=True)

def _silu(x):
    return jax.nn.silu(x)

def _sigmoid(x):
    return jax.nn.sigmoid(x)

def _layernorm(x, axis=-1, eps=1e-05):
    m = jnp.mean(x, axis=axis, keepdims=True)
    v = jnp.var(x, axis=axis, keepdims=True)
    return (x - m) / jnp.sqrt(v + eps)

def _scatter_add(tgt, idx, src, axis=0):
    return tgt.at[idx].add(src)

def _segment_sum(src, seg, n):
    return jax.ops.segment_sum(src, seg, n)
kernel_name = 'mk_macaron_d1_jaxref_r4_d8c627'

def setup_inputs(seed: int=0):
    np.random.seed(seed)
    _w = jnp.asarray

    def _L0_attn_setup():
        import jax, jax.numpy as jnp
        import numpy as np
        D, E, N, D_DELTA, D_CONV = (512, 1024, 16, 128, 4)
        B_SZ, L = (1, 512)
        EPS = 1e-05

        def _silu(x):
            return x * jax.nn.sigmoid(x)
        key = jax.random.key(seed)
        ks = jax.random.split(key, 16)
        s = lambda k, shape, scale: jax.random.normal(k, shape, dtype=jnp.float32) * scale
        return {'resid': s(ks[0], (B_SZ, L, D), 1.0), 'norm_w': jnp.ones((D,), jnp.float32), 'W_skip': s(ks[1], (D, E), D ** (-0.5)), 'W_in': s(ks[2], (D, E), D ** (-0.5)), 'conv_w': s(ks[3], (D_CONV, 1, E), D_CONV ** (-0.5)), 'conv_b': s(ks[4], (E,), 0.02), 'W_delta_1': s(ks[5], (E, D_DELTA), E ** (-0.5)), 'W_delta_2': s(ks[6], (D_DELTA, E), D_DELTA ** (-0.5)), 'b_delta_2': s(ks[7], (E,), 0.02), 'W_B': s(ks[8], (E, N), E ** (-0.5)), 'W_C': s(ks[9], (E, N), E ** (-0.5)), 'A_log': s(ks[10], (E, N), 0.5), 'W_D': jnp.ones((E,), jnp.float32), 'W_out': s(ks[11], (E, D), E ** (-0.5))}
    _L0_attn_in = _L0_attn_setup()

    def _L0_ffn_setup():
        import jax, jax.numpy as jnp
        import numpy as np
        D_MODEL = 512
        D_EXPERT = 2048
        EPS = 1e-08

        def ternary_quant(w):
            scale = jnp.mean(jnp.abs(w)) + EPS
            q = jnp.clip(jnp.round(w / scale), -1.0, 1.0) * scale
            return w + jax.lax.stop_gradient(q - w)
        key = jax.random.key(seed)
        k_x, k_up, k_gate, k_down = jax.random.split(key, 4)
        std_in = 1.0 / np.sqrt(D_MODEL)
        std_exp = 1.0 / np.sqrt(D_EXPERT)
        return {'x': jax.random.normal(k_x, (4, 512, D_MODEL), dtype=jnp.float32), 'W_up': jax.random.normal(k_up, (D_EXPERT, D_MODEL), dtype=jnp.float32) * std_in, 'W_gate': jax.random.normal(k_gate, (D_EXPERT, D_MODEL), dtype=jnp.float32) * std_in, 'W_down': jax.random.normal(k_down, (D_MODEL, D_EXPERT), dtype=jnp.float32) * std_exp}
    _L0_ffn_in = _L0_ffn_setup()
    _d = {'L0_attn_resid': _L0_attn_in['resid'], 'L0_attn_norm_w': _L0_attn_in['norm_w'], 'L0_attn_W_skip': _L0_attn_in['W_skip'], 'L0_attn_W_in': _L0_attn_in['W_in'], 'L0_attn_conv_w': _L0_attn_in['conv_w'], 'L0_attn_conv_b': _L0_attn_in['conv_b'], 'L0_attn_W_delta_1': _L0_attn_in['W_delta_1'], 'L0_attn_W_delta_2': _L0_attn_in['W_delta_2'], 'L0_attn_b_delta_2': _L0_attn_in['b_delta_2'], 'L0_attn_W_B': _L0_attn_in['W_B'], 'L0_attn_W_C': _L0_attn_in['W_C'], 'L0_attn_A_log': _L0_attn_in['A_log'], 'L0_attn_W_D': _L0_attn_in['W_D'], 'L0_attn_W_out': _L0_attn_in['W_out'], 'L0_ffn_W_up': _L0_ffn_in['W_up'], 'L0_ffn_W_gate': _L0_ffn_in['W_gate'], 'L0_ffn_W_down': _L0_ffn_in['W_down']}
    _x0 = _d['L0_attn_resid']
    _d['L0_attn_resid'] = jax.random.normal(jax.random.fold_in(jax.random.key(seed), 1), (4, 1024, 512), dtype=_x0.dtype)
    del _x0
    return _d

def reference(L0_attn_resid, L0_attn_norm_w, L0_attn_W_skip, L0_attn_W_in, L0_attn_conv_w, L0_attn_conv_b, L0_attn_W_delta_1, L0_attn_W_delta_2, L0_attn_b_delta_2, L0_attn_W_B, L0_attn_W_C, L0_attn_A_log, L0_attn_W_D, L0_attn_W_out, L0_ffn_W_up, L0_ffn_W_gate, L0_ffn_W_down):

    def _L0_attn_ref(resid, norm_w, W_skip, W_in, conv_w, conv_b, W_delta_1, W_delta_2, b_delta_2, W_B, W_C, A_log, W_D, W_out):
        import jax, jax.numpy as jnp
        import numpy as np
        D, E, N, D_DELTA, D_CONV = (512, 1024, 16, 128, 4)
        B_SZ, L = (1, 512)
        EPS = 1e-05

        def _silu(x):
            return x * jax.nn.sigmoid(x)
        resid_norm = resid * jax.lax.rsqrt(jnp.mean(resid * resid, axis=-1, keepdims=True) + EPS) * norm_w
        skip = resid_norm @ W_skip
        x_in = resid_norm @ W_in
        conv = jax.lax.conv_general_dilated(x_in, conv_w, window_strides=(1,), padding=[(D_CONV - 1, 0)], dimension_numbers=('NWC', 'WIO', 'NWC'), feature_group_count=E)
        x = _silu(conv + conv_b)
        delta = jax.nn.softplus(x @ W_delta_1 @ W_delta_2 + b_delta_2)
        Bm = x @ W_B
        Cm = x @ W_C
        A = -jnp.exp(A_log)

        def step(h, inp):
            d_l, B_l, C_l, x_l = inp
            A_bar = jnp.exp(d_l[:, :, None] * A)
            h = h * A_bar + (d_l * x_l)[:, :, None] * B_l[:, None, :]
            y_l = jnp.einsum('ben,bn->be', h, C_l)
            return (h, y_l)
        h0 = jnp.zeros((resid.shape[0], E, N), x.dtype)
        xs = (jnp.swapaxes(delta, 0, 1), jnp.swapaxes(Bm, 0, 1), jnp.swapaxes(Cm, 0, 1), jnp.swapaxes(x, 0, 1))
        _, ys = jax.lax.scan(step, h0, xs)
        y = jnp.swapaxes(ys, 0, 1)
        y_apply_D = y + x * W_D
        y_skip = y_apply_D * _silu(skip)
        return resid + y_skip @ W_out

    def _L0_ffn_ref(x, W_up, W_gate, W_down):
        import jax, jax.numpy as jnp
        import numpy as np
        D_MODEL = 512
        D_EXPERT = 2048
        EPS = 1e-08

        def ternary_quant(w):
            scale = jnp.mean(jnp.abs(w)) + EPS
            q = jnp.clip(jnp.round(w / scale), -1.0, 1.0) * scale
            return w + jax.lax.stop_gradient(q - w)
        wu = ternary_quant(W_up)
        wg = ternary_quant(W_gate)
        wd = ternary_quant(W_down)
        up = jnp.einsum('bsd,ed->bse', x, wu)
        gate = jnp.einsum('bsd,ed->bse', x, wg)
        hidden = jax.nn.silu(up) * gate
        return jnp.einsum('bse,de->bsd', hidden, wd)
    x = L0_attn_resid
    x = x + 0.5 * _L0_ffn_ref(_layernorm(x, axis=-1), L0_ffn_W_up, L0_ffn_W_gate, L0_ffn_W_down)
    x = x + _L0_attn_ref(_layernorm(x, axis=-1), L0_attn_norm_w, L0_attn_W_skip, L0_attn_W_in, L0_attn_conv_w, L0_attn_conv_b, L0_attn_W_delta_1, L0_attn_W_delta_2, L0_attn_b_delta_2, L0_attn_W_B, L0_attn_W_C, L0_attn_A_log, L0_attn_W_D, L0_attn_W_out)
    x = x + 0.5 * _L0_ffn_ref(_layernorm(x, axis=-1), L0_ffn_W_up, L0_ffn_W_gate, L0_ffn_W_down)
    return x

_drawn_inputs = setup_inputs


def setup_inputs(seed=0):
    import zlib

    import numpy as np

    out = dict(_drawn_inputs(seed))
    spreads = {'L0_attn_norm_w': (1.0, 0.2), 'L0_attn_W_D': (1.0, 0.2)}
    factors = {'L0_attn_conv_b': 4.817, 'L0_attn_b_delta_2': 8.0}
    for name, (base, spread) in spreads.items():
        noise = np.random.default_rng([zlib.crc32(name.encode()), seed]).standard_normal(out[name].shape)
        drawn = base * np.exp(spread * noise) if base else spread * noise
        out[name] = jnp.asarray(drawn.astype(out[name].dtype))
    for name, factor in factors.items():
        out[name] = (out[name] * factor).astype(out[name].dtype)
    return out
```

```python
import numpy as np

import concourse.bass as bass
from concourse import mybir
from contextlib import ExitStack

P = 128
D, E, F, N, DD = 512, 1024, 2048, 16, 128
B, L = 4, 1024
TAPS = 4
TOK = B * L
CH = 256
TB = CH // P
NCH = TOK // CH
CPB = L // CH
DB, EB, FB = D // P, E // P, F // P
HE = EB // 2
STEPS = 2 * N
PAIRS = FB // 2
XSLOTS = 4
EPS = 1e-5
TEPS = 1e-8
XN_SCALE = 1024.0
HID_SCALE = 2.0 ** -24

SLOTS = [
    [("D2_1", 0)],
    [("YT_1", 0)],
    [("T1", 0), ("UT_1", 0)],
    [("UG1_0", 0), ("OM", 0)],
    [("OM", 1)],
    [("UG1_1", 0), ("OM", 2)],
    [("OM", 3)],
    [("UG1_2", 0), ("UG1_3", 0)],
    [("UG1_4", 0)],
    [("UG1_5", 0), ("UG1_6", 0)],
    [("UG1_7", 0)],
    [("SK_0", 0)],
    [("SK_0", 1), ("SK_1", 0)],
    [("SK_1", 1)],
    [("DN1", 0), ("T2", 0)],
    [("DN1", 1)],
    [("DN1", 2)],
    [("DN1", 3)],
    [("UG2_0", 0), ("UG2_1", 0)],
    [("YT_0", 0), ("UG2_2", 0)],
    [("Tp", 0), ("UG2_3", 0)],
    [("IN_0", 0), ("IN_0", 1)],
    [("UG2_4", 0)],
    [("IN_1", 0), ("IN_1", 1)],
    [("UG2_5", 0), ("UG2_6", 0)],
    [("UG2_7", 0)],
    [],
    [("D1", 0), ("BC", 0)],
    [("D2_0", 0), ("DN2", 0)],
    [("DN2", 1)],
    [("DN2", 2)],
    [("UT_0", 0), ("DN2", 3)],
]
PREV = {"YT_1", "OM", "T2", "DN2"} | {f"UG2_{p}" for p in range(PAIRS)}
THIS = {"D2_1", "UT_1", "SK_0", "SK_1", "YT_0"}
NEXT = {"T1", "DN1", "Tp", "IN_0", "IN_1", "D1", "BC", "D2_0", "UT_0"} | {f"UG1_{p}" for p in range(PAIRS)}
ORDER = []
SLOT_OF = {}
for _s, _pieces in enumerate(SLOTS):
    for _name, _q in _pieces:
        if _name not in ORDER:
            ORDER.append(_name)
        SLOT_OF[_name] = _s
PHASES = {"fill": NEXT, "first": THIS | NEXT, "loop": PREV | THIS | NEXT, "last": PREV | THIS, "drain": PREV}
JOBS = {ph: [n for n in ORDER if n in has] for ph, has in PHASES.items()}
LOOP_JOBS = len(JOBS["loop"])
FIRST_NO = {"fill": 0}
FIRST_NO["first"] = len(JOBS["fill"])
FIRST_NO["loop"] = FIRST_NO["first"] + len(JOBS["first"]) - LOOP_JOBS
FIRST_NO["last"] = FIRST_NO["loop"] + LOOP_JOBS * (NCH - 1)
FIRST_NO["drain"] = FIRST_NO["last"] + len(JOBS["last"])
assert LOOP_JOBS % 2 == 0
for _ph in ("first", "loop", "last"):
    for _a, _b in zip(JOBS[_ph], JOBS[_ph][2:]):
        _first = min(_s for _s, _pieces in enumerate(SLOTS) if (_b, 0) in _pieces)
        assert _first > SLOT_OF[_a], (_ph, _a, _b)
assert all(JOBS[ph][-1] == "UT_0" for ph in ("fill", "first", "loop"))


def job_no(ph, i, name):
    no = FIRST_NO[ph] + JOBS[ph].index(name)
    before = no // 2
    return no % 2, (before + (LOOP_JOBS // 2) * i if ph == "loop" else before)


def last_job(ph, i):
    no = FIRST_NO[ph] - 1
    before = no // 2
    return no % 2, (before + (LOOP_JOBS // 2) * i if ph == "loop" else before)


def ffn_run(ph, i, kind):
    if ph == "fill":
        return 0
    if ph == "first":
        return 1
    return 2 * i + (kind - 1) if ph == "loop" else (2 * NCH - 2 if ph == "last" else 2 * NCH - 1)


def ln_run(ph, i, kind):
    if ph in ("fill", "first"):
        return {"fill": 0, "first": 2}[ph] + {"1": 0, "p": 1}[kind]
    if ph == "loop":
        return 3 * i + 1 + {"1": 0, "2": 1, "p": 2}[kind]
    return 3 * NCH - 2 + (0 if ph == "last" else 1)


def need(eng, sem, value):
    if isinstance(value, int) and value <= 0:
        return
    eng.wait_ge(sem, value)


def macaron_kernel(nc, resid, norm_w, W_skip, W_in, conv_w, conv_b, W_delta_1, W_delta_2, b_delta_2, W_B, W_C,
                   A_log, W_D, W_out, W_up, W_gate, W_down, out):
    f32, f16, f8, i32 = mybir.dt.float32, mybir.dt.float16, mybir.dt.float8e4, mybir.dt.int32
    ACT = mybir.ActivationFunctionType
    ALU = mybir.AluOpType
    AX = mybir.AxisListType

    x_dram = resid.rearrange("b l d -> (b l) d").rearrange("(c t p) d -> c p t d", t=TB, p=P)
    out_dram = out.rearrange("b l d -> (b l) d").rearrange("(c t p) d -> c p t d", t=TB, p=P)

    ctx = ExitStack()
    with ctx:
        def sb(name, shape, dt=f32, where=ctx):
            return where.enter_context(nc.sbuf_tensor(name, shape, dt))

        def sem(name):
            return ctx.enter_context(nc.semaphore(name))

        qT = [sb("q_up", [P, DB, F], f8), sb("q_gate", [P, DB, F], f8), sb("q_down", [P, FB, D], f8)]
        q_up, q_gate, q_down = qT
        w_in = sb("w_in", [P, DB, E])
        w_skip = sb("w_skip", [P, DB, E])
        w_out = sb("w_out", [P, EB, D])
        w_d1 = sb("w_d1", [P, EB, DD])
        w_d2 = sb("w_d2", [P, E])
        w_bc = sb("w_bc", [P, EB, 2 * N])
        a_neg = sb("a_neg", [P, EB, N])
        NV = DB + TAPS * EB + 3 * EB
        vrow = sb("vrow", [NV, P])
        vcol = sb("vcol", [P, NV])
        nw = vcol[:, 0:DB]
        cw = vcol[:, DB:DB + TAPS * EB]
        cb = vcol[:, DB + TAPS * EB:DB + (TAPS + 1) * EB]
        b2 = vcol[:, DB + (TAPS + 1) * EB:DB + (TAPS + 2) * EB]
        wd = vcol[:, DB + (TAPS + 2) * EB:NV]
        ident = sb("ident", [P, P])
        ident16 = sb("ident16", [P, P], f16)
        ones = sb("ones", [P, P])
        keep = sb("keep", [P, NCH], i32)
        eps_c = sb("eps_c", [P, TB])
        mhalf_c = sb("mhalf_c", [P, TB])
        scale_c = sb("scale_c", [P, TB])
        asum = sb("asum", [P, 3, 4])
        asum1 = sb("asum1", [P, 3])
        wscale = sb("wscale", [P, 3])
        thr = sb("thr", [P, 2, 3])
        tanh_sc = sb("tanh_sc", [P, 1])
        prod_sc = sb("prod_sc", [P, 2])
        down_sc = sb("down_sc", [P, 1])
        xs = sb("xs", [P, XSLOTS, TB, D])
        carry = sb("carry", [P, STEPS * HE])
        hist = sb("hist", [P, 2, HE, TAPS - 1])
        st = sb("st", [P, TB, 6])
        mv = sb("mv", [P, TB, 2])
        rt = sb("rt", [P, 6, TB])

        early = ExitStack()
        with early:
            wraw = [sb(f"wraw{m}", [P, F * D // P], f32, early) for m in range(3)]
            qh = w_out[:, :, :].rearrange("p e d -> p (e d)").bitcast(f16).rearrange("p (r n) -> p r n", r=2)

        xn_cin = sb("xn_cin", [P, HE * (TAPS - 1 + CH)])
        xn = xn_cin[:, 0:TB * D].rearrange("p (t d) -> p t d", t=TB)
        cin = xn_cin[:, :].rearrange("p (e t) -> p e t", e=HE)
        xh = sb("xh", [P, DB, CH], f16)
        xl = sb("xl", [P, DB, CH], f16)
        act = sb("act", [P, 2, 2 * CH])
        hh = sb("hh", [P, FB, CH], f16)
        hl = sb("hl", [P, FB, CH], f16)
        xrT = sb("xrT", [P, DB, CH])
        tmp = sb("tmp", [P, HE * CH])
        tmp_h = tmp[:, :].rearrange("p (e t) -> p e t", e=HE)
        xr = tmp[:, :].rearrange("p (t d) -> p t d", t=TB)
        xc = sb("xc", [P, EB, CH])
        xw = sb("xw", [P, HE, CH])
        gz = sb("gz", [P, EB, CH])
        d1 = sb("d1", [P, CH])
        bcn = sb("bcn", [P, TB, 2 * N])
        bcur = sb("bcur", [P, TB, N])
        ccur = sb("ccur", [P, TB, N])
        delta = sb("delta", [P, EB, CH])
        uT = sb("uT", [P, TB, E])
        abar = sb("abar", [P, 2, HE, CH])
        ub = sb("ub", [P, 2, TB, HE * P])
        h = sb("h", [P, 2, HE, CH])
        y = sb("y", [P, TB, E])

        ps = ctx.enter_context(nc.psum_tensor("ps", [P, 8, 512], f32))
        ubT = ps[:, 0:2, :]
        hT = ps[:, 2:4, :]
        pair = [ps[:, 4:6, :], ps[:, 6:8, :]]

        x_loaded, out_stored = sem("x_loaded"), sem("out_stored")
        raw_loaded = [sem(f"raw_loaded{m}") for m in range(3)]
        vec_loaded, alog_loaded = sem("vec_loaded"), sem("alog_loaded")
        win_loaded, wsk_loaded, wout_loaded = sem("win_loaded"), sem("wsk_loaded"), sem("wout_loaded")
        wd1_loaded, wd2_loaded, wbc_loaded = sem("wd1_loaded"), sem("wd2_loaded"), sem("wbc_loaded")
        const_zero, const_ready, dve_const = sem("const_zero"), sem("const_ready"), sem("dve_const")
        abs_ready, asum_ready, asums_ready = sem("abs_ready"), sem("asum_ready"), sem("asums_ready")
        scale_step, gt_ready, q_ready = sem("scale_step"), sem("gt_ready"), sem("q_ready")
        qt_ready, q_saved = sem("qt_ready"), sem("q_saved")
        vec_ready, vcol_ready, vec_step = sem("vec_ready"), sem("vcol_ready"), sem("vec_step")
        a_exp, a_done = sem("a_exp"), sem("a_done")
        pair_ready = [sem("pair_ready0"), sem("pair_ready1")]
        pair_used = [sem("pair_used0"), sem("pair_used1")]
        ub_ready, ubT_ready, abar_ready = sem("ub_ready"), sem("ubT_ready"), sem("abar_ready")
        scanned, hT_ready = sem("scanned"), sem("hT_ready")
        y_added = [sem("y_added0"), sem("y_added1")]
        carry_saved, carry_ready = sem("carry_saved"), sem("carry_ready")
        b_copied, c_copied = sem("b_copied"), sem("c_copied")
        ln_stats, ln_moments, xn_ready = sem("ln_stats"), sem("ln_moments"), sem("xn_ready")
        rstd_step, rms_step = sem("rstd_step"), sem("rms_step")
        xr_ready, x12_ready = sem("xr_ready"), sem("x12_ready")
        xh_ready, tanh_ready, silu_ready = sem("xh_ready"), sem("tanh_ready"), sem("silu_ready")
        hh_ready, hl_ready = sem("hh_ready"), sem("hl_ready")
        hist_step, conv_step = sem("hist_step"), sem("conv_step")
        ctanh_ready, xc_ready, xw_ready = sem("ctanh_ready"), sem("xc_ready"), sem("xw_ready")
        sp_step, delta_ready, u_ready = sem("sp_step"), sem("delta_ready"), sem("u_ready")
        gtanh_ready, yw_ready, z_ready = sem("gtanh_ready"), sem("yw_ready"), sem("z_ready")
        uT_half = sem("uT_half")
        pool_go, dve_go = sem("pool_go"), sem("dve_go")
        pe_go, sp_go = sem("pe_go"), sem("sp_go")

        NQ = 6
        QB = 4

        block = ctx.enter_context(nc.Block())

        def phases(eng, run):
            run("fill", -1)
            run("first", 0)
            with eng.Fori(1, NCH - 1) as i:
                run("loop", i)
            run("last", NCH - 1)
            run("drain", NCH)

        def at_slot(names, lag):
            table = {}
            for name in ORDER:
                if name in names:
                    table.setdefault(SLOT_OF[name] + lag, []).append(name)
            return table

        @block.sync
        def _(sp):
            sp.dma_start(vrow[0:DB, :], norm_w.rearrange("(r p) -> r p", p=P)).then_inc(vec_loaded, 16)
            o = DB
            sp.dma_start(vrow[o:o + TAPS * EB, :], conv_w.rearrange("k o (r p) -> (k o r) p", p=P)).then_inc(vec_loaded, 16)
            o += TAPS * EB
            for v in (conv_b, b_delta_2, W_D):
                sp.dma_start(vrow[o:o + EB, :], v.rearrange("(r p) -> r p", p=P)).then_inc(vec_loaded, 16)
                o += EB
            sp.dma_start(wraw[0][:, :].rearrange("p (f d) -> p f d", d=D),
                         W_up.rearrange("(f p) d -> p f d", p=P)).then_inc(raw_loaded[0], 16)
            sp.dma_start(wraw[1][:, :].rearrange("p (f d) -> p f d", d=D),
                         W_gate.rearrange("(f p) d -> p f d", p=P)).then_inc(raw_loaded[1], 16)
            sp.dma_start(xs[:, 0, :, :], x_dram[0]).then_inc(x_loaded, 16)
            sp.dma_start(wraw[2][:, :].rearrange("p (r f) -> p r f", f=F),
                         W_down.rearrange("(r p) f -> p r f", p=P)).then_inc(raw_loaded[2], 16)
            sp.dma_start(a_neg[:, :, :], A_log.rearrange("(e p) n -> p e n", p=P)).then_inc(alog_loaded, 16)
            sp.dma_start(w_in[:, :, :], W_in.rearrange("(d p) e -> p d e", p=P)).then_inc(win_loaded, 16)
            sp.dma_start(w_d1[:, :, :], W_delta_1.rearrange("(e p) r -> p e r", p=P)).then_inc(wd1_loaded, 16)
            sp.dma_start(w_bc[:, :, 0:N], W_B.rearrange("(e p) n -> p e n", p=P)).then_inc(wbc_loaded, 16)
            sp.dma_start(w_bc[:, :, N:2 * N], W_C.rearrange("(e p) n -> p e n", p=P)).then_inc(wbc_loaded, 16)
            sp.dma_start(w_d2[:, :], W_delta_2).then_inc(wd2_loaded, 16)
            sp.dma_start(w_skip[:, :, :], W_skip.rearrange("(d p) e -> p d e", p=P)).then_inc(wsk_loaded, 16)
            sp.wait_ge(q_saved, NQ * QB)
            sp.dma_start(w_out[:, :, :], W_out.rearrange("(e p) d -> p e d", p=P)).then_inc(wout_loaded, 16)

            def load_x(c):
                sp.wait_ge(x_loaded, 16 * c)
                sp.dma_start(xs[:, bass.ds(c % XSLOTS, 1), :, :].rearrange("p s t d -> p (s t) d"),
                             x_dram[bass.ds(c, 1)].rearrange("s p t d -> p (s t) d")).then_inc(x_loaded, 16)

            def store(ph, i):
                pr, before = job_no(ph, i, "DN2")
                sp.wait_ge(pair_used[pr], before + 1)
                sp.sem_inc(sp_go, 1)
                sp.dma_start(out_dram[bass.ds(i - 1, 1)].rearrange("s p t d -> p (s t) d"),
                             xs[:, bass.ds((i - 1) % XSLOTS, 1), :, :].rearrange("p s t d -> p (s t) d")
                             ).then_inc(out_stored, 16)
                sp.wait_ge(out_stored, 16 * i)
                sp.sem_inc(sp_go, 1)

            def run(ph, i):
                if ph == "fill":
                    load_x(1)
                if ph in ("first", "loop"):
                    if ph == "first":
                        load_x(2)
                    else:
                        sp.wait_ge(x_loaded, 16 * i + 32)
                        sp.sem_inc(sp_go, 1)
                        with_next = i + 2
                        sp.dma_start(xs[:, bass.ds(with_next % XSLOTS, 1), :, :].rearrange("p s t d -> p (s t) d"),
                                     x_dram[bass.ds(with_next % NCH, 1)].rearrange("s p t d -> p (s t) d")
                                     ).then_inc(x_loaded, 16)
                if ph in ("loop", "last", "drain"):
                    store(ph, i)

            phases(sp, run)
            sp.wait_ge(out_stored, 16 * NCH)

        @block.gpsimd
        def _(pool):
            def go():
                pool.sem_inc(pool_go, 1)

            pl = nc.gpsimd
            pl.memset(ident[:, :], 0.0).then_inc(const_zero, 1)
            pl.memset(ident16[:, :], 0.0).then_inc(const_zero, 1)
            pl.memset(ones[:, :], 1.0)
            pl.memset(eps_c[:, :], EPS)
            pl.memset(mhalf_c[:, :], -0.5)
            pl.memset(scale_c[:, :], XN_SCALE)
            pool.wait_ge(const_zero, 2)
            pl.affine_select(out=ident[:, :], in_=ident[:, :], compare_op=ALU.not_equal, fill=1.0, base=0,
                             pattern=[[-1, P]], channel_multiplier=1).then_inc(const_ready, 1)
            pl.affine_select(out=ident16[:, :], in_=ident16[:, :], compare_op=ALU.not_equal, fill=1.0, base=0,
                             pattern=[[-1, P]], channel_multiplier=1).then_inc(const_ready, 1)
            pool.wait_ge(a_exp, 1)
            pl.tensor_scalar(a_neg[:, :, :], a_neg[:, :, :], -1.0, None, ALU.mult).then_inc(a_done, 1)
            pool.wait_ge(vec_step, 2)
            pool.wait_ge(q_saved, NQ * QB)

            def u_times_b(ph, i, s):
                S, half, n = STEPS * i + s, s // N, s % N
                if s == 0:
                    need(pool, delta_ready, 2 * i + 1)
                    go()
                    pl.tensor_copy(bcur[:, :, :], bcn[:, :, 0:N]).then_inc(b_copied, 1)
                    need(pool, b_copied, i + 1)
                    pr, before = last_job(ph, i)
                    need(pool, pair_used[pr], before + 1)
                if s == N:
                    pr, before = job_no(ph, i, "UT_1")
                    need(pool, pair_used[pr], before + 1)
                need(pool, ubT_ready, 2 * S - 2)
                go()
                for t in range(TB):
                    pl.tensor_scalar(ub[:, s % 2, t, :], uT[:, t, half * HE * P:(half + 1) * HE * P],
                                     bcur[:, t, n:n + 1], None, ALU.mult).then_inc(ub_ready, 1)

            def save_carry(i, s):
                S = STEPS * i + s
                need(pool, scanned, 2 * S + 2)
                go()
                pl.tensor_copy(carry[:, HE * s:HE * (s + 1)], h[:, s % 2, :, CH - 1]).then_inc(carry_saved, 1)

            def rstd(ph, i, kind):
                r = ffn_run(ph, i, kind)
                need(pool, ln_moments, TB * ln_run(ph, i, str(kind)) + TB)
                pl.tensor_tensor(rt[:, 0, :], mv[:, :, 1], eps_c[:, :], ALU.add).then_inc(rstd_step, 1)
                need(pool, rstd_step, 3 * r + 1)
                pl.tensor_tensor(rt[:, 1, :], rt[:, 0, :], mhalf_c[:, :], ALU.pow).then_inc(rstd_step, 1)
                need(pool, rstd_step, 3 * r + 2)
                pl.tensor_tensor(rt[:, 2, :], rt[:, 1, :], scale_c[:, :], ALU.mult).then_inc(rstd_step, 1)

            def rms(ph, i):
                k = i + 1
                need(pool, ln_moments, TB * ln_run(ph, i, "p") + TB)
                pl.tensor_tensor(rt[:, 0, :], mv[:, :, 1], eps_c[:, :], ALU.add).then_inc(rms_step, 1)
                need(pool, rms_step, 6 * k + 1)
                pl.tensor_tensor(rt[:, 1, :], rt[:, 0, :], mhalf_c[:, :], ALU.pow).then_inc(rms_step, 1)
                need(pool, rms_step, 6 * k + 2)
                pl.tensor_tensor(rt[:, 3, :], rt[:, 1, :], rt[:, 1, :], ALU.mult).then_inc(rms_step, 1)
                need(pool, rms_step, 6 * k + 3)
                pl.tensor_tensor(rt[:, 4, :], rt[:, 3, :], mv[:, :, 1], ALU.mult).then_inc(rms_step, 1)
                need(pool, rms_step, 6 * k + 4)
                pl.tensor_tensor(rt[:, 3, :], rt[:, 4, :], eps_c[:, :], ALU.add).then_inc(rms_step, 1)
                need(pool, rms_step, 6 * k + 5)
                pl.tensor_tensor(rt[:, 5, :], rt[:, 3, :], mhalf_c[:, :], ALU.pow).then_inc(rms_step, 1)

            def x12(ph, i):
                k = i + 1
                need(pool, xn_ready, TB * ln_run(ph, i, "p") + TB)
                go()
                slot = k % XSLOTS
                pl.tensor_tensor(xs[:, slot, :, :], xs[:, slot, :, :], xn[:, :, :], ALU.add).then_inc(x12_ready, 1)

            def hidden_low(ph, i, kind, p):
                g = PAIRS * ffn_run(ph, i, kind) + p
                need(pool, hh_ready, g + 1)
                pl.tensor_tensor(hl[:, 2 * p:2 * p + 2, :], act[:, p % 2, :].rearrange("q (f t) -> q f t", f=2),
                                 hh[:, 2 * p:2 * p + 2, :], ALU.subtract).then_inc(hl_ready, 1)

            def u_of(c, half):
                need(pool, delta_ready, 2 * c + half + 1)
                need(pool, xc_ready, 2 * c + half + 1)
                pl.tensor_tensor(tmp_h, delta[:, half * HE:(half + 1) * HE, :], xc[:, half * HE:(half + 1) * HE, :],
                                 ALU.mult).then_inc(u_ready, 1)

            def x_times_d(i, half):
                need(pool, z_ready, 2 * i + half)
                need(pool, xc_ready, 2 * i + half + 1)
                go()
                for e in range(HE):
                    b = half * HE + e
                    ins = pl.tensor_scalar(xw[:, e, :], xc[:, b, :], wd[:, b:b + 1], None, ALU.mult)
                ins.then_inc(xw_ready, 1)

            hl_at = at_slot([f"UG{k}_{p}" for k in (1, 2) for p in range(PAIRS)], 2)

            def run(ph, i):
                has = PHASES[ph]
                scan = "SK_0" in has
                for s in range(STEPS + 2):
                    if scan and s < STEPS:
                        u_times_b(ph, i, s)
                    if scan and 1 <= s <= STEPS:
                        save_carry(i, s - 1)
                    if s == 0 and "T1" in has:
                        rstd(ph, i, 1)
                    if s == SLOT_OF["D2_1"] + 1 and scan:
                        u_of(i, 1)
                    if s == SLOT_OF["OM"] + 1 and "OM" in has:
                        rstd(ph, i, 2)
                    for name in hl_at.get(s, ()):
                        if name in has:
                            hidden_low(ph, i, int(name[2]), int(name[4]))
                    if s == 10 and scan:
                        x_times_d(i, 0)
                    if s == SLOT_OF["DN1"] + 1 and "DN1" in has:
                        rms(ph, i)
                    if s == SLOT_OF["DN1"] + 2 and "DN1" in has:
                        x12(ph, i)
                    if s == SLOT_OF["YT_0"] + 2 and scan:
                        x_times_d(i, 1)
                    if s == SLOT_OF["D2_0"] + 1 and "D2_0" in has:
                        u_of(i + 1, 0)

            phases(pool, run)

        @block.scalar
        def _(sc):
            ac = nc.scalar

            junk = ps[:, 0:4, :].rearrange("p a b -> p (a b)")
            for m in range(3):
                sc.wait_ge(raw_loaded[m], 16)
                for q in range(4):
                    if 4 * m + q:
                        sc.wait_ge(abs_ready, 4 * m + q)
                    ac.activation(junk, wraw[m][:, q * F:(q + 1) * F], ACT.Abs,
                                  accum_out=asum[:, m, q:q + 1]).then_inc(abs_ready, 1)
            sc.wait_ge(alog_loaded, 16)
            ac.activation(a_neg[:, :, :], a_neg[:, :, :], ACT.Exp).then_inc(a_exp, 1)

            def save_q(hb):
                m, part = hb // 2, hb % 2
                for b in range(QB):
                    sc.wait_ge(qt_ready, QB * hb + b + 1)
                    src = ps[:, 4 + b, :].bitcast(f16)
                    if m < 2:
                        ac.activation(qT[m][:, b, part * (F // 2):(part + 1) * (F // 2)], src, ACT.Copy,
                                      saturate=False).then_inc(q_saved, 1)
                    else:
                        ac.activation(q_down[:, 4 * b:4 * b + 4, part * (D // 2):(part + 1) * (D // 2)],
                                      src.rearrange("p (f d) -> p f d", f=4), ACT.Copy,
                                      saturate=False).then_inc(q_saved, 1)

            for hb in range(NQ):
                save_q(hb)
            sc.wait_ge(vec_step, 2)
            sc.wait_ge(a_done, 1)
            sc.wait_ge(q_saved, NQ * QB)

            def exps(ph, i, s):
                S, half, n = STEPS * i + s, s // N, s % N
                if n == 0:
                    need(sc, delta_ready, 2 * i + half + 1)
                for b in range(2):
                    need(sc, scanned, 2 * (S - 2) + b + 1)
                    for e in (2 * b, 2 * b + 1):
                        k = half * HE + e
                        ins = ac.activation(abar[:, s % 2, e, :], delta[:, k, :], ACT.Exp, scale=a_neg[:, k, n:n + 1])
                    ins.then_inc(abar_ready, 1)

            def ready(ph, i, name):
                pr, before = job_no(ph, i, name)
                need(sc, pair_ready[pr], before + 1)
                return pr, pair[pr]

            def flat(pp):
                return pp.rearrange("p a b -> p (a b)")

            def x_high(ph, i, kind):
                pr, pp = ready(ph, i, f"T{kind}")
                ac.activation(xh[:, :, :].rearrange("p d t -> p (d t)"), flat(pp), ACT.Copy).then_inc(xh_ready, 1)

            def tanh_up(ph, i, kind, p):
                g = PAIRS * ffn_run(ph, i, kind) + p
                need(sc, hl_ready, g - 1)
                pr, pp = ready(ph, i, f"UG{kind}_{p}")
                ac.activation(act[:, p % 2, :], pp[:, 0, :], ACT.Tanh, scale=tanh_sc[:, 0:1]).then_inc(tanh_ready, 1)

            def hidden_high(ph, i, kind, p):
                pr, before = job_no(ph, i, f"UG{kind}_{p}")
                need(sc, pair_used[pr], before + 1)
                ac.activation(hh[:, 2 * p:2 * p + 2, :], act[:, p % 2, :].rearrange("q (f t) -> q f t", f=2),
                              ACT.Copy).then_inc(hh_ready, 1)

            def x_norm_T(ph, i):
                pr, pp = ready(ph, i, "Tp")
                for d in range(DB):
                    ins = ac.activation(xrT[:, d, :], flat(pp)[:, d * CH:(d + 1) * CH], ACT.Copy, scale=nw[:, d:d + 1])
                ins.then_inc(pair_used[pr], 1)

            def conv_in(ph, i, half):
                need(sc, conv_step, 22 * (2 * (i + 1) + half))
                need(sc, x12_ready, i + 2)
                pr, pp = ready(ph, i, f"IN_{half}")
                ac.activation(cin[:, :, TAPS - 1:], flat(pp).rearrange("p (e t) -> p e t", e=HE),
                              ACT.Copy).then_inc(pair_used[pr], 1)

            def conv_tanh(i, half):
                c = i + 1
                need(sc, conv_step, 22 * (2 * c + half) + 22)
                need(sc, xc_ready, 2 * c + half)
                ac.activation(tmp_h, xc[:, half * HE:(half + 1) * HE, :], ACT.Tanh).then_inc(ctanh_ready, 1)

            def delta_rank(ph, i):
                pr, pp = ready(ph, i, "D1")
                ac.activation(d1[:, :], pp[:, 0, 0:CH], ACT.Copy).then_inc(pair_used[pr], 1)

            def b_and_c(ph, i):
                need(sc, b_copied, i + 1)
                need(sc, c_copied, i + 1)
                pr, pp = ready(ph, i, "BC")
                ac.activation(bcn[:, :, :], pp[:, 0, 0:TB * 2 * N].rearrange("p (t n) -> p t n", t=TB),
                              ACT.Copy).then_inc(pair_used[pr], 1)

            def softplus(ph, i, half):
                c = i + 1 if half == 0 else i
                g = 4 * (2 * c + half)
                pr, pp = ready(ph, i, f"D2_{half}")
                for e in range(HE):
                    b = half * HE + e
                    ins = ac.activation(delta[:, b, :], flat(pp)[:, e * CH:(e + 1) * CH], ACT.Identity, bias=b2[:, b:b + 1])
                ins.then_inc(pair_used[pr], 1)
                need(sc, pair_used[pr], job_no(ph, i, f"D2_{half}")[1] + 1)
                v = delta[:, half * HE:(half + 1) * HE, :]
                ac.activation(tmp_h, v, ACT.Abs).then_inc(sp_step, 1)
                need(sc, sp_step, 3 * (2 * c + half) + 1)
                ac.activation(tmp_h, tmp_h, ACT.Exp, scale=-1.0).then_inc(sp_step, 1)
                need(sc, sp_step, 3 * (2 * c + half) + 2)
                ac.activation(tmp_h, tmp_h, ACT.Ln, bias=1.0).then_inc(sp_step, 1)

            def u_T(ph, i, half):
                c = i + 1 if half == 0 else i
                need(sc, ub_ready, TB * (STEPS * (c - 1) + N * (half + 1)))
                pr, pp = ready(ph, i, f"UT_{half}")
                ac.activation(uT[:, :, half * HE * P:(half + 1) * HE * P], pp, ACT.Copy).then_inc(pair_used[pr], 1)

            def skip_tanh(ph, i, half):
                pr, pp = ready(ph, i, f"SK_{half}")
                ac.activation(gz[:, half * HE:(half + 1) * HE, :].rearrange("p e t -> p (e t)"), flat(pp), ACT.Tanh,
                              scale=0.5).then_inc(gtanh_ready, 1)

            ug = [f"UG{k}_{p}" for k in (1, 2) for p in range(PAIRS)]
            hh_at, tanh_at = at_slot(ug, 2), at_slot(ug, 1)

            def run(ph, i):
                has = PHASES[ph]
                scan = "SK_0" in has

                def after(name, lag, s):
                    return name in has and s == SLOT_OF[name] + lag

                for s in range(STEPS + 2):
                    if scan and s < STEPS:
                        exps(ph, i, s)
                    for name in hh_at.get(s, ()):
                        if name in has:
                            hidden_high(ph, i, int(name[2]), int(name[4]))
                    for half in range(2):
                        if after(f"IN_{half}", 2, s):
                            conv_tanh(i, half)
                    for name in ORDER:
                        if not after(name, 1, s):
                            continue
                        if name[:2] == "UG":
                            tanh_up(ph, i, int(name[2]), int(name[4]))
                        elif name in ("T1", "T2"):
                            x_high(ph, i, int(name[1]))
                        elif name == "Tp":
                            x_norm_T(ph, i)
                        elif name[:2] == "IN":
                            conv_in(ph, i, int(name[3]))
                        elif name == "D1":
                            delta_rank(ph, i)
                        elif name == "BC":
                            b_and_c(ph, i)
                        elif name[:2] == "D2":
                            softplus(ph, i, int(name[3]))
                        elif name[:2] == "UT":
                            u_T(ph, i, int(name[3]))
                        elif name[:2] == "SK":
                            skip_tanh(ph, i, int(name[3]))

            phases(sc, run)

        @block.vector
        def _(ve):
            v = nc.vector

            def go():
                ve.sem_inc(dve_go, 1)

            v.memset(keep[:, :], -1).then_inc(dve_const, 1)
            ve.wait_ge(dve_const, 1)
            for b in range(B):
                v.memset(keep[:, b * CPB:b * CPB + 1], 0).then_inc(dve_const, 1)
            v.memset(carry[:, :], 0.0).then_inc(dve_const, 1)
            v.memset(hist[:, :, :, :], 0.0).then_inc(dve_const, 1)
            ve.wait_ge(dve_const, B + 3)

            ve.wait_ge(vec_ready, 1)
            v.tensor_copy(vcol[:, :], ps[:, 7, 0:NV]).then_inc(vcol_ready, 1)
            ve.wait_ge(vcol_ready, 1)
            v.tensor_scalar(vcol[:, DB:DB + (TAPS + 1) * EB], vcol[:, DB:DB + (TAPS + 1) * EB], 0.5, None,
                            ALU.mult).then_inc(vec_step, 1)
            for m in range(3):
                ve.wait_ge(abs_ready, 4 * (m + 1))
                v.reduce_sum(asum1[:, m:m + 1], asum[:, m, :], AX.X).then_inc(asum_ready, 1)
                ve.wait_ge(asums_ready, m + 1)
                v.tensor_scalar(wscale[:, m:m + 1], ps[:, 6, m:m + 1], 1.0 / (F * D), TEPS, ALU.mult,
                                ALU.add).then_inc(scale_step, 1)
                ve.wait_ge(scale_step, 3 * m + 1)
                v.tensor_scalar(thr[:, 0, m:m + 1], wscale[:, m:m + 1], 0.5, None, ALU.mult).then_inc(scale_step, 1)
                v.tensor_scalar(thr[:, 1, m:m + 1], wscale[:, m:m + 1], -0.5, None, ALU.mult).then_inc(scale_step, 1)
                ve.wait_ge(scale_step, 3 * m + 3)
                half_len = F * D // P // 2
                for part in range(2):
                    hb = 2 * m + part
                    if hb >= 2:
                        ve.wait_ge(qt_ready, QB * (hb - 1))
                    src = wraw[m][:, part * half_len:(part + 1) * half_len]
                    v.tensor_scalar(qh[:, hb % 2, :], src, thr[:, 0, m:m + 1], None, ALU.is_gt).then_inc(gt_ready, 1)
                    ve.wait_ge(gt_ready, hb + 1)
                    v.scalar_tensor_tensor(out=qh[:, hb % 2, :], in0=src, scalar=thr[:, 1, m:m + 1],
                                           in1=qh[:, hb % 2, :], op0=ALU.is_lt, op1=ALU.subtract).then_inc(q_ready, 1)
            v.tensor_scalar(tanh_sc[:, :], wscale[:, 0:1], -0.5 / XN_SCALE, None, ALU.mult).then_inc(vec_step, 1)
            v.tensor_tensor(prod_sc[:, 0:1], wscale[:, 0:1], wscale[:, 1:2], ALU.mult).then_inc(scale_step, 1)
            ve.wait_ge(scale_step, 10)
            v.tensor_tensor(prod_sc[:, 1:2], prod_sc[:, 0:1], wscale[:, 2:3], ALU.mult).then_inc(scale_step, 1)
            ve.wait_ge(scale_step, 11)
            v.tensor_scalar(down_sc[:, :], prod_sc[:, 1:2], -0.5 * 0.5 / (HID_SCALE * XN_SCALE * XN_SCALE), None,
                            ALU.mult).then_inc(scale_step, 1)
            ve.wait_ge(scale_step, 12)
            ve.wait_ge(a_done, 1)
            ve.wait_ge(q_saved, NQ * QB)

            def ready(ph, i, name):
                pr, before = job_no(ph, i, name)
                need(ve, pair_ready[pr], before + 1)
                return pr, pair[pr]

            def flat(pp):
                return pp.rearrange("p a b -> p (a b)")

            def start_chunk(i):
                need(ve, carry_saved, STEPS * i)
                v.tensor_tensor(carry[:, :].bitcast(i32), carry[:, :].bitcast(i32),
                                keep[:, i:i + 1].broadcast_to([P, STEPS * HE]) if isinstance(i, int) else
                                keep[:, bass.ds(i, 1)].broadcast_to([P, STEPS * HE]),
                                ALU.bitwise_and).then_inc(carry_ready, 1)
                need(ve, delta_ready, 2 * i + 1)
                for t in range(TB):
                    need(ve, y_added[t], STEPS * i)
                go()
                v.tensor_copy(ccur[:, :, :], bcn[:, :, N:2 * N]).then_inc(c_copied, 1)
                need(ve, carry_ready, i + 1)

            def scans(i, s):
                S = STEPS * i + s
                need(ve, hT_ready, 2 * S - 2)
                need(ve, carry_saved, S - 1)
                for b in range(2):
                    need(ve, abar_ready, 2 * S + b + 1)
                    need(ve, ubT_ready, 2 * S + b + 1)
                    for e in range(2):
                        k = 2 * b + e
                        ins = v.tensor_tensor_scan(h[:, s % 2, k, :], abar[:, s % 2, k, :], ubT[:, b, e * CH:(e + 1) * CH],
                                                   carry[:, HE * s + k:HE * s + k + 1], ALU.mult, ALU.add)
                    ins.then_inc(scanned, 1)

            def y_add(i, s):
                S, half, n = STEPS * i + s, s // N, s % N
                if s == 0:
                    need(ve, c_copied, i + 1)
                for t in range(TB):
                    need(ve, hT_ready, 2 * S + t + 1)
                    yy = y[:, t, half * HE * P:(half + 1) * HE * P]
                    cc = ccur[:, t, n:n + 1]
                    if n == 0:
                        ins = v.tensor_scalar(yy, hT[:, t, :], cc, None, ALU.mult)
                    else:
                        need(ve, y_added[t], S)
                        ins = v.scalar_tensor_tensor(out=yy, in0=hT[:, t, :], scalar=cc, in1=yy, op0=ALU.mult, op1=ALU.add)
                    ins.then_inc(y_added[t], 1)

            def moments(ph, i, kind, slot):
                l = ln_run(ph, i, kind)
                go()
                for t in range(TB):
                    v.bn_stats(st[:, t, :], xs[:, slot, t, :]).then_inc(ln_stats, 1)
                need(ve, ln_stats, TB * l + TB)
                go()
                for t in range(TB):
                    v.bn_aggr(mv[:, t, :], st[:, t, :]).then_inc(ln_moments, 1)

            def normalise(ph, i, kind, slot):
                row = 2
                if kind == "p":
                    row = 1
                    need(ve, rms_step, 6 * (i + 1) + 6)
                else:
                    need(ve, rstd_step, 3 * ffn_run(ph, i, int(kind)) + 3)
                l = ln_run(ph, i, kind)
                for t in range(TB):
                    v.tensor_scalar(xn[:, t, :], xs[:, slot, t, :], mv[:, t, 0:1], rt[:, row, t:t + 1], ALU.subtract,
                                    ALU.mult).then_inc(xn_ready, 1)

            def rms_scaled(ph, i):
                if "UT_1" in PHASES[ph]:
                    pr, before = job_no(ph, i, "UT_1")
                    need(ve, pair_ready[pr], before + 1)
                need(ve, xn_ready, TB * ln_run(ph, i, "p") + TB)
                for t in range(TB):
                    ins = v.tensor_scalar(xr[:, t, :], xn[:, t, :], rt[:, 5, t:t + 1], None, ALU.mult)
                ins.then_inc(xr_ready, 1)

            def x_low(ph, i, kind):
                need(ve, xh_ready, ffn_run(ph, i, kind) + 1)
                pr, pp = ready(ph, i, f"T{kind}")
                v.tensor_tensor(xl[:, :, :].rearrange("p d t -> p (d t)"), flat(pp), xh[:, :, :].rearrange("p d t -> p (d t)"),
                                ALU.subtract).then_inc(pair_used[pr], 1)

            def hidden(ph, i, kind, p):
                g = PAIRS * ffn_run(ph, i, kind) + p
                need(ve, tanh_ready, g + 1)
                pr, pp = ready(ph, i, f"UG{kind}_{p}")
                a = act[:, p % 2, :]
                v.scalar_tensor_tensor(out=a, in0=a, scalar=1.0, in1=pp[:, 0, :], op0=ALU.add, op1=ALU.mult).then_inc(silu_ready, 1)
                need(ve, silu_ready, g + 1)
                v.scalar_tensor_tensor(out=a, in0=pp[:, 1, :], scalar=HID_SCALE, in1=a, op0=ALU.mult,
                                       op1=ALU.mult).then_inc(pair_used[pr], 1)

            def add_to_stream(ph, i, name, slot, factor):
                pr, pp = ready(ph, i, name)
                for t in range(TB):
                    xx = xs[:, slot, t, :]
                    ins = v.scalar_tensor_tensor(out=xx, in0=pp[:, t, :], scalar=factor, in1=xx, op0=ALU.mult, op1=ALU.add)
                ins.then_inc(pair_used[pr], 1)
                need(ve, pair_used[pr], job_no(ph, i, name)[1] + 1)

            def conv(ph, i, half):
                c = i + 1
                g = 22 * (2 * c + half)
                pr, before = job_no(ph, i, f"IN_{half}")
                need(ve, conv_step, g)
                need(ve, x12_ready, c + 1)
                pt, tb = job_no(ph, i, "Tp")
                need(ve, pair_ready[pt], tb + 1)
                v.tensor_tensor(cin[:, :, 0:TAPS - 1].bitcast(i32), hist[:, half, :, :].bitcast(i32),
                                (keep[:, c:c + 1] if isinstance(c, int) else keep[:, bass.ds(c, 1)])
                                .unsqueeze(2).broadcast_to([P, HE, TAPS - 1]), ALU.bitwise_and).then_inc(conv_step, 1)
                need(ve, pair_used[pr], before + 1)
                need(ve, conv_step, g + 1)
                need(ve, xw_ready, 2 * c - 1 + half)
                v.tensor_copy(hist[:, half, :, :], cin[:, :, CH:CH + TAPS - 1]).then_inc(conv_step, 1)
                for tap in range(TAPS):
                    if tap:
                        need(ve, conv_step, g + 2 + HE * tap)
                    for e in range(HE):
                        b = half * HE + e
                        w = cw[:, tap * EB + b:tap * EB + b + 1]
                        src = cin[:, e, tap:tap + CH]
                        if tap == 0:
                            ins = v.tensor_scalar(xc[:, b, :], src, w, cb[:, b:b + 1], ALU.mult, ALU.add)
                        else:
                            ins = v.scalar_tensor_tensor(out=xc[:, b, :], in0=src, scalar=w, in1=xc[:, b, :],
                                                         op0=ALU.mult, op1=ALU.add)
                        ins.then_inc(conv_step, 1)
                for _ in range(22 - 2 - TAPS * HE):
                    ve.sem_inc(conv_step, 1)

            def conv_silu(i, half):
                c = i + 1
                need(ve, ctanh_ready, 2 * c + half + 1)
                xx = xc[:, half * HE:(half + 1) * HE, :]
                v.scalar_tensor_tensor(out=xx, in0=tmp_h, scalar=1.0, in1=xx, op0=ALU.add, op1=ALU.mult).then_inc(xc_ready, 1)

            def softplus(c, half):
                need(ve, sp_step, 3 * (2 * c + half) + 3)
                dd = delta[:, half * HE:(half + 1) * HE, :]
                v.scalar_tensor_tensor(out=dd, in0=dd, scalar=0.0, in1=tmp_h, op0=ALU.max, op1=ALU.add).then_inc(delta_ready, 1)

            def skip_gate(ph, i, half):
                need(ve, gtanh_ready, 2 * i + half + 1)
                pr, pp = ready(ph, i, f"SK_{half}")
                gg = gz[:, half * HE:(half + 1) * HE, :].rearrange("p e t -> p (e t)")
                v.scalar_tensor_tensor(out=gg, in0=gg, scalar=1.0, in1=flat(pp), op0=ALU.add, op1=ALU.mult).then_inc(pair_used[pr], 1)

            def gated(ph, i, half):
                c = i if half == 0 else i - 1
                need(ve, xw_ready, 2 * c + half + 1)
                pr, pp = ready(ph, i, f"YT_{half}")
                ww = xw[:, :, :].rearrange("p e t -> p (e t)")
                gg = gz[:, half * HE:(half + 1) * HE, :].rearrange("p e t -> p (e t)")
                v.tensor_tensor(ww, flat(pp), ww, ALU.add).then_inc(pair_used[pr], 1)
                need(ve, pair_used[pr], job_no(ph, i, f"YT_{half}")[1] + 1)
                v.tensor_tensor(gg, ww, gg, ALU.mult).then_inc(z_ready, 1)

            def run(ph, i):
                has = PHASES[ph]
                scan = "SK_0" in has
                nslot = (i + 1) % XSLOTS
                pslot = (i - 1) % XSLOTS

                def after(name, lag, s):
                    return name in has and s == SLOT_OF[name] + lag

                if scan:
                    start_chunk(i)
                for s in range(STEPS + 3):
                    if scan and s < STEPS:
                        scans(i, s)
                    if scan and 1 <= s <= STEPS:
                        y_add(i, s - 1)
                    if s == 0 and "T1" in has:
                        need(ve, x_loaded, 16 * (i + 2))
                        moments(ph, i, "1", nslot)
                    if s == 1 and "T1" in has:
                        normalise(ph, i, "1", nslot)
                    if after("OM", 2, s):
                        if "Tp" in has:
                            need(ve, x12_ready, i + 1)
                        normalise(ph, i, "2", pslot)
                    if after("DN1", 2, s):
                        if "T2" in has:
                            pr, before = job_no(ph, i, "T2")
                            need(ve, pair_ready[pr], before + 1)
                        normalise(ph, i, "p", nslot)
                        rms_scaled(ph, i)
                    for half in range(2):
                        if after(f"IN_{half}", 2, s):
                            conv_silu(i, half)
                    for name in ORDER:
                        if not after(name, 1, s):
                            continue
                        if name[:2] == "UG":
                            hidden(ph, i, int(name[2]), int(name[4]))
                        elif name in ("T1", "T2"):
                            x_low(ph, i, int(name[1]))
                        elif name == "OM":
                            add_to_stream(ph, i, "OM", pslot, 0.5)
                            moments(ph, i, "2", pslot)
                        elif name == "DN1":
                            add_to_stream(ph, i, "DN1", nslot, down_sc[:, 0:1])
                            moments(ph, i, "p", nslot)
                        elif name == "DN2":
                            add_to_stream(ph, i, "DN2", pslot, down_sc[:, 0:1])
                        elif name[:2] == "IN":
                            conv(ph, i, int(name[3]))
                        elif name[:2] == "D2":
                            softplus(i + 1 if name == "D2_0" else i, int(name[3]))
                        elif name[:2] == "SK":
                            skip_gate(ph, i, int(name[3]))
                        elif name[:2] == "YT":
                            gated(ph, i, int(name[3]))

            phases(ve, run)

        @block.tensor
        def _(pe):
            te = nc.tensor

            pe.wait_ge(const_ready, 2)
            pe.wait_ge(vec_loaded, 16 * 5)
            te.transpose(ps[:, 7, 0:NV], vrow[:, :], ident[0:NV, 0:NV]).then_inc(vec_ready, 1)
            pe.wait_ge(vcol_ready, 1)
            for m in range(3):
                pe.wait_ge(asum_ready, m + 1)
                if m:
                    pe.wait_ge(q_saved, QB * 2 * m)
                te.matmul(ps[:, 6, m:m + 1], ones[:, :], asum1[:, m:m + 1], start=True, stop=True).then_inc(asums_ready, 1)
                for part in range(2):
                    hb = 2 * m + part
                    pe.wait_ge(q_ready, hb + 1)
                    if hb:
                        pe.wait_ge(q_saved, QB * hb)
                    src = qh[:, hb % 2, :]
                    for b in range(QB):
                        bank = ps[:, 4 + b, :].bitcast(f16)
                        for j in range(8):
                            if m < 2:
                                blk = src[:, j * D + b * P:j * D + (b + 1) * P]
                            else:
                                f, d = 4 * b + j // 2, j % 2
                                blk = src[:, d * F + f * P:d * F + (f + 1) * P]
                            ins = te.transpose(bank[:, j * P:(j + 1) * P], blk, ident16[:, :])
                        ins.then_inc(qt_ready, 1)
            pe.wait_ge(q_saved, NQ * QB)
            for sm, n in ((win_loaded, 1), (wd1_loaded, 1), (wbc_loaded, 2), (wd2_loaded, 1), (wsk_loaded, 1), (wout_loaded, 1)):
                pe.wait_ge(sm, 16 * n)

            def inputs_T(i, s):
                S = STEPS * i + s
                need(pe, ub_ready, TB * S + TB)
                for b in range(2):
                    need(pe, scanned, 2 * (S - 1) + b + 1)
                    for e in range(2):
                        for t in range(TB):
                            ins = te.transpose(ubT[:, b, e * CH + t * P:e * CH + (t + 1) * P],
                                               ub[:, s % 2, t, (2 * b + e) * P:(2 * b + e + 1) * P], ident[:, :])
                    ins.then_inc(ubT_ready, 1)

            def states_T(i, s):
                S = STEPS * i + s
                need(pe, scanned, 2 * S + 2)
                for t in range(TB):
                    need(pe, y_added[t], S)
                    for e in range(HE):
                        ins = te.transpose(hT[:, t, e * P:(e + 1) * P], h[:, s % 2, e, t * P:(t + 1) * P], ident[:, :])
                    ins.then_inc(hT_ready, 1)

            def opened(ph, i, name, piece=0):
                pr, before = job_no(ph, i, name)
                if piece == 0:
                    need(pe, pair_used[pr], before)
                return pr, pair[pr]

            def flat(pp):
                return pp.rearrange("p a b -> p (a b)")

            def used(ph, i, name):
                pr, before = job_no(ph, i, name)
                need(pe, pair_used[pr], before + 1)

            def rows_T(ph, i, name, src):
                pr, pp = opened(ph, i, name)
                for d in range(DB):
                    for t in range(TB):
                        ins = te.transpose(flat(pp)[:, d * CH + t * P:d * CH + (t + 1) * P], src[:, t, d * P:(d + 1) * P],
                                           ident[:, :])
                ins.then_inc(pair_ready[pr], 1)

            def up_gate(ph, i, kind, p):
                name = f"UG{kind}_{p}"
                pr, pp = opened(ph, i, name)
                if p == 0:
                    used(ph, i, f"T{kind}")
                pe.sem_inc(pe_go, 1)
                for b, w in enumerate((q_up, q_gate)):
                    for f in range(2):
                        col = (2 * p + f) * P
                        for d in range(DB):
                            for part in (xh, xl):
                                ins = te.matmul(pp[:, b, f * CH:(f + 1) * CH], w[:, d, col:col + P], part[:, d, :],
                                                start=(d == 0 and part is xh), stop=(d == DB - 1 and part is xl))
                ins.then_inc(pair_ready[pr], 1)

            def down(ph, i, kind, piece):
                name = f"DN{kind}"
                pr, pp = opened(ph, i, name, piece)
                need(pe, hl_ready, PAIRS * ffn_run(ph, i, kind) + 2 * piece + 2)
                pe.sem_inc(pe_go, 1)
                for t in range(TB):
                    for f in range(4 * piece, 4 * piece + 4):
                        for part in (hh, hl):
                            ins = te.matmul(pp[:, t, :], part[:, f, t * P:(t + 1) * P], q_down[:, f, :],
                                            start=(f == 0 and part is hh), stop=(f == FB - 1 and part is hl))
                if piece == 3:
                    ins.then_inc(pair_ready[pr], 1)

            def project(ph, i, name, w, piece):
                half = int(name[3])
                pr, pp = opened(ph, i, name, piece)
                for e in (2 * piece, 2 * piece + 1):
                    col = (half * HE + e) * P
                    for d in range(DB):
                        ins = te.matmul(flat(pp)[:, e * CH:(e + 1) * CH], w[:, d, col:col + P], xrT[:, d, :],
                                        start=(d == 0), stop=(d == DB - 1))
                if piece == 1:
                    ins.then_inc(pair_ready[pr], 1)

            def delta_1(ph, i):
                need(pe, xc_ready, 2 * (i + 1) + 2)
                pr, pp = opened(ph, i, "D1")
                for e in range(EB):
                    ins = te.matmul(pp[:, 0, 0:CH], w_d1[:, e, :], xc[:, e, :], start=(e == 0), stop=(e == EB - 1))
                ins.then_inc(pair_ready[pr], 1)

            def b_and_c(ph, i):
                pr, pp = opened(ph, i, "BC")
                for t in range(TB):
                    for e in range(EB):
                        ins = te.matmul(pp[:, 0, t * 2 * N:(t + 1) * 2 * N], xc[:, e, t * P:(t + 1) * P], w_bc[:, e, :],
                                        start=(e == 0), stop=(e == EB - 1))
                ins.then_inc(pair_ready[pr], 1)

            def delta_2(ph, i, half):
                pr, pp = opened(ph, i, f"D2_{half}")
                if half == 0:
                    used(ph, i, "D1")
                for e in range(HE):
                    col = (half * HE + e) * P
                    ins = te.matmul(flat(pp)[:, e * CH:(e + 1) * CH], w_d2[:, col:col + P], d1[:, :], start=True, stop=True)
                ins.then_inc(pair_ready[pr], 1)

            def u_T(ph, i, half):
                c = i + 1 if half == 0 else i
                need(pe, u_ready, 2 * c + half + 1)
                pr, pp = opened(ph, i, f"UT_{half}")
                for t in range(TB):
                    for e in range(HE):
                        ins = te.transpose(pp[:, t, e * P:(e + 1) * P], tmp_h[:, e, t * P:(t + 1) * P], ident[:, :])
                ins.then_inc(pair_ready[pr], 1)

            def y_T(ph, i, half):
                c = i if half == 0 else i - 1
                for t in range(TB):
                    need(pe, y_added[t], STEPS * c + N * (half + 1))
                pr, pp = opened(ph, i, f"YT_{half}")
                for e in range(HE):
                    col = (half * HE + e) * P
                    for t in range(TB):
                        ins = te.transpose(flat(pp)[:, e * CH + t * P:e * CH + (t + 1) * P], y[:, t, col:col + P], ident[:, :])
                ins.then_inc(pair_ready[pr], 1)

            def out_proj(ph, i, piece):
                pr, pp = opened(ph, i, "OM", piece)
                if piece == 0:
                    need(pe, z_ready, 2 * i)
                for t in range(TB):
                    for e in (2 * piece, 2 * piece + 1):
                        ins = te.matmul(pp[:, t, :], gz[:, e, t * P:(t + 1) * P], w_out[:, e, :],
                                        start=(e == 0), stop=(e == EB - 1))
                if piece == 3:
                    ins.then_inc(pair_ready[pr], 1)

            def job(ph, i, name, piece):
                if name[:2] == "UG":
                    up_gate(ph, i, int(name[2]), int(name[4]))
                elif name[:2] == "DN":
                    down(ph, i, int(name[2]), piece)
                elif name in ("T1", "T2"):
                    need(pe, xn_ready, TB * ln_run(ph, i, name[1]) + TB)
                    rows_T(ph, i, name, xn)
                elif name == "Tp":
                    need(pe, xr_ready, i + 2)
                    rows_T(ph, i, name, xr)
                elif name[:2] == "IN":
                    used(ph, i, "Tp")
                    project(ph, i, name, w_in, piece)
                elif name[:2] == "SK":
                    project(ph, i, name, w_skip, piece)
                elif name == "D1":
                    delta_1(ph, i)
                elif name == "BC":
                    b_and_c(ph, i)
                elif name[:2] == "D2":
                    delta_2(ph, i, int(name[3]))
                elif name[:2] == "UT":
                    u_T(ph, i, int(name[3]))
                elif name[:2] == "YT":
                    y_T(ph, i, int(name[3]))
                else:
                    out_proj(ph, i, piece)

            def run(ph, i):
                has = PHASES[ph]
                scan = "SK_0" in has
                for s in range(STEPS):
                    if scan:
                        inputs_T(i, s)
                    for name, piece in SLOTS[s]:
                        if name in has:
                            job(ph, i, name, piece)
                    if scan:
                        states_T(i, s)

            phases(pe, run)


_ORDER = ['resid', 'norm_w', 'W_skip', 'W_in', 'conv_w', 'conv_b', 'W_delta_1', 'W_delta_2', 'b_delta_2', 'W_B', 'W_C',
          'A_log', 'W_D', 'W_out']
_INS = [f'L0_attn_{n}' for n in _ORDER] + ['L0_ffn_W_up', 'L0_ffn_W_gate', 'L0_ffn_W_down']


def kernel(**inputs):
    import numpy as _np
    import concourse.bacc as _bacc
    from concourse import mybir as _mybir
    from concourse.bass_utils import run_bass_kernel_spmd as _run

    nc = _bacc.Bacc("TRN2", target_bir_lowering=False, num_devices=1)
    arrays, args = {}, []
    for name in _INS:
        a = _np.ascontiguousarray(inputs[name])
        arrays[f"in_{name}_dram"] = a
        args.append(nc.dram_tensor(f"in_{name}_dram", a.shape, _mybir.dt.from_np(a.dtype), kind="ExternalInput").ap())
    o = nc.dram_tensor("out_dram", (B, L, D), _mybir.dt.float32, kind="ExternalOutput").ap()
    macaron_kernel(nc, *args, o)
    r = _run(nc, [arrays], core_ids=[0])
    return r.results[0]["out_dram"]
```

```python
import numpy as np

import concourse.bass as bass
from concourse import mybir
from contextlib import ExitStack

P = 128
D, E, F, N, DD = 512, 1024, 2048, 16, 128
B, L = 4, 1024
TAPS = 4
TOK = B * L
CH = 256
TB = CH // P
NCH = TOK // CH
CPB = L // CH
DB, EB, FB = D // P, E // P, F // P
HE = EB // 2
CONV_STEPS = 2 + (TAPS - 1) * HE
STEPS = 2 * N
PAIRS = FB // 2
XSLOTS = 4
EPS = 1e-5
TEPS = 1e-8
XN_SCALE = 1024.0
HID_SCALE = 2.0 ** -24

PARTS = {"OM": EB, "DN1": FB, "DN2": FB, "SK_0": HE, "SK_1": HE, "IN_0": HE, "IN_1": HE}
PLANES = 4
BBS = STEPS // PLANES
SLOTS = [
    ["D2_1", "T1", ("OM", 0, 1)],
    ["YT_1", "BB_1", ("OM", 1, 3)],
    ["UG1_0", ("OM", 3, 4)],
    [("OM", 4, 7)],
    [("OM", 7, 8), "UG1_1"],
    ["BB_2", "UG1_2"],
    ["UG1_3", ("SK_0", 0, 1)],
    ["UG1_4", ("SK_0", 1, 2)],
    ["UG1_5", ("SK_0", 2, 3)],
    ["BB_3", "UG1_6"],
    ["UG1_7", ("SK_0", 3, 4)],
    [("DN1", 0, 6)],
    ["T2", ("DN1", 6, 11)],
    ["BB_4", ("DN1", 11, 16)],
    ["UG2_0", ("SK_1", 0, 1)],
    [("SK_1", 1, 4)],
    ["Tp", "BB_5", "UG2_1"],
    ["YT_0", ("IN_0", 0, 2)],
    [("IN_0", 2, 4)],
    ["UG2_2"],
    ["BB_6", ("IN_1", 0, 2)],
    [("IN_1", 2, 4)],
    ["UG2_3"],
    ["UG2_4"],
    ["BB_7", "UG2_5"],
    ["D1", "BC"],
    ["UG2_6"],
    ["D2_0", "UG2_7"],
    [("DN2", 0, 4)],
    ["BB_0", ("DN2", 4, 8)],
    [("DN2", 8, 12)],
    [("DN2", 12, 16)],
]
SLOTS = [[j if isinstance(j, tuple) else (j, 0, 1) for j in jobs] for jobs in SLOTS]
PREV = {"YT_1", "OM", "T2", "DN2"} | {f"UG2_{p}" for p in range(PAIRS)}
THIS = {"D2_1", "SK_0", "SK_1", "YT_0"} | {f"BB_{q}" for q in range(1, BBS)}
NEXT = {"T1", "DN1", "Tp", "IN_0", "IN_1", "D1", "BC", "D2_0", "BB_0"} | {f"UG1_{p}" for p in range(PAIRS)}
ORDER = []
SLOT_OF = {}
EARLY = set()
PAIR_OF = {}
NPAIR = 3
AHEAD = 2
RING = 3
NEXT_LN = 26
_owner, _end = [None] * NPAIR, [-NPAIR + p for p in range(NPAIR)]
for _s, _pieces in enumerate(SLOTS):
    for _name, _lo, _hi in _pieces:
        if _lo == 0:
            _p = min((p for p in range(NPAIR) if _owner[p] is None), key=lambda p: _end[p])
            assert _end[_p] < _s, (_name, "waits for the consumer of a job in its own slot")
            ORDER.append(_name)
            PAIR_OF[_name], _owner[_p] = _p, _name
        if _hi == PARTS.get(_name, 1):
            SLOT_OF[_name] = _s
            _p = PAIR_OF[_name]
            _owner[_p], _end[_p] = None, _s
            if _name != _pieces[-1][0]:
                EARLY.add(_name)
USE_OF = {n: SLOT_OF[n] + (n not in EARLY) for n in ORDER}
assert set(ORDER) == PREV | THIS | NEXT and len(SLOTS) == STEPS
PHASES = {"fill": NEXT, "first": THIS | NEXT, "loop": PREV | THIS | NEXT, "last": PREV | THIS, "drain": PREV}
JOBS = {(ph, p): [n for n in ORDER if n in has and PAIR_OF[n] == p] for ph, has in PHASES.items() for p in range(NPAIR)}


def job_no(ph, i, name):
    p = PAIR_OF[name]
    size = {f: len(JOBS[f, p]) for f in PHASES}
    before = JOBS[ph, p].index(name)
    if ph != "fill":
        before += size["fill"]
    if ph == "loop":
        before = before + size["first"] - size["loop"] + size["loop"] * i
    elif ph in ("last", "drain"):
        before += size["first"] + size["loop"] * (NCH - 2) + (size["last"] if ph == "drain" else 0)
    return p, before


def ring_lag(s):
    return RING if s >= STEPS % RING else STEPS % RING


def ffn_run(ph, i, kind):
    if ph == "fill":
        return 0
    if ph == "first":
        return 1
    return 2 * i + (kind - 1) if ph == "loop" else (2 * NCH - 2 if ph == "last" else 2 * NCH - 1)


def ln_run(ph, i, kind):
    if ph in ("fill", "first"):
        return {"fill": 0, "first": 2}[ph] + {"1": 0, "p": 1, "n": 2}[kind]
    if ph == "loop":
        return 3 * i + {"1": 1, "2": 2, "p": 3, "n": 4}[kind]
    return 3 * NCH - 1 + (0 if ph == "last" else 1)


def rstd_run(ph, i, kind):
    if ph in ("fill", "first"):
        return {"fill": 0, "first": 1}[ph] + {"1": 0, "n": 1}[kind]
    if ph == "loop":
        return 2 * i + {"1": 0, "2": 1, "n": 2}[kind]
    return 2 * NCH - 1 + (0 if ph == "last" else 1)


def need(eng, sem, value):
    if isinstance(value, int) and value <= 0:
        return
    eng.wait_ge(sem, value)


def macaron_kernel(nc, resid, norm_w, W_skip, W_in, conv_w, conv_b, W_delta_1, W_delta_2, b_delta_2, W_B, W_C,
                   A_log, W_D, W_out, W_up, W_gate, W_down, out):
    f32, f16, f8, i32 = mybir.dt.float32, mybir.dt.float16, mybir.dt.float8e4, mybir.dt.int32
    ACT = mybir.ActivationFunctionType
    ALU = mybir.AluOpType
    AX = mybir.AxisListType

    x_dram = resid.rearrange("b l d -> (b l) d").rearrange("(c t p) d -> c p t d", t=TB, p=P)
    out_dram = out.rearrange("b l d -> (b l) d").rearrange("(c t p) d -> c p t d", t=TB, p=P)

    ctx = ExitStack()
    with ctx:
        def sb(name, shape, dt=f32, where=ctx):
            return where.enter_context(nc.sbuf_tensor(name, shape, dt))

        def sem(name):
            return ctx.enter_context(nc.semaphore(name))

        qT = [sb("q_up", [P, DB, F], f8), sb("q_gate", [P, DB, F], f8), sb("q_down", [P, FB, D], f8)]
        q_up, q_gate, q_down = qT
        w_in = sb("w_in", [P, DB, E])
        w_skip = sb("w_skip", [P, DB, E])
        w_out = sb("w_out", [P, EB, D])
        w_d1 = sb("w_d1", [P, EB, DD])
        w_d2 = sb("w_d2", [P, E])
        w_bc = sb("w_bc", [P, EB, 2 * N])
        a_neg = sb("a_neg", [P, EB, N])
        NV = DB + TAPS * EB + 3 * EB
        vrow = sb("vrow", [NV, P])
        vcol = sb("vcol", [P, NV])
        nw = vcol[:, 0:DB]
        cw = vcol[:, DB:DB + TAPS * EB]
        cb = vcol[:, DB + TAPS * EB:DB + (TAPS + 1) * EB]
        b2 = vcol[:, DB + (TAPS + 1) * EB:DB + (TAPS + 2) * EB]
        wd = vcol[:, DB + (TAPS + 2) * EB:NV]
        ident = sb("ident", [P, P])
        ident16 = sb("ident16", [P, P], f16)
        ones = sb("ones", [P, P])
        keep = sb("keep", [P, NCH], i32)
        eps_c = sb("eps_c", [P, TB])
        mhalf_c = sb("mhalf_c", [P, TB])
        scale_c = sb("scale_c", [P, TB])
        asum = sb("asum", [P, 3, 4])
        asum1 = sb("asum1", [P, 3])
        wscale = sb("wscale", [P, 3])
        thr = sb("thr", [P, 2, 3])
        tanh_sc = sb("tanh_sc", [P, 1])
        prod_sc = sb("prod_sc", [P, 2])
        down_sc = sb("down_sc", [P, 1])
        xs = sb("xs", [P, XSLOTS, TB, D])
        carry = sb("carry", [P, STEPS * HE])
        hist = sb("hist", [P, 2, HE, TAPS - 1])
        st = sb("st", [P, TB, 6])
        mv = sb("mv", [P, TB, 2])
        rt = sb("rt", [P, 6, TB])

        early = ExitStack()
        with early:
            wraw = [sb(f"wraw{m}", [P, F * D // P], f32, early) for m in range(3)]
            qh = w_out[:, :, :].rearrange("p e d -> p (e d)").bitcast(f16).rearrange("p (r n) -> p r n", r=2)

        xn_cin = sb("xn_cin", [P, HE * (TAPS - 1 + CH)])
        xn = xn_cin[:, 0:TB * D].rearrange("p (t d) -> p t d", t=TB)
        cin = xn_cin[:, :].rearrange("p (e t) -> p e t", e=HE)
        xh = sb("xh", [P, DB, CH], f16)
        xl = sb("xl", [P, DB, CH], f16)
        act = sb("act", [P, 2, 2 * CH])
        hh = sb("hh", [P, FB, CH], f16)
        hl = sb("hl", [P, FB, CH], f16)
        xrT = sb("xrT", [P, DB, CH])
        tmp = sb("tmp", [P, HE * CH])
        tmp_h = tmp[:, :].rearrange("p (e t) -> p e t", e=HE)
        xr = tmp[:, :].rearrange("p (t d) -> p t d", t=TB)
        xc = sb("xc", [P, EB, CH])
        xw = sb("xw", [P, HE, CH])
        gz = sb("gz", [P, EB, CH])
        d1 = sb("d1", [P, CH])
        bcn = sb("bcn", [P, TB, 2 * N])
        ccur = sb("ccur", [P, TB, N])
        delta = sb("delta", [P, EB, CH])
        u = sb("u", [P, HE, CH])
        bb = sb("bb", [P, 2, PLANES, CH])
        abar = sb("abar", [P, RING, HE, 1 + CH])
        h = sb("h", [P, RING, HE, 1 + CH])
        y = sb("y", [P, TB, HE * P])

        ps = ctx.enter_context(nc.psum_tensor("ps", [P, 8, 512], f32))
        hT = ps[:, 0:2, :]
        pair = [ps[:, 2 + 2 * p:4 + 2 * p, :] for p in range(NPAIR)]

        x_loaded, out_stored = sem("x_loaded"), sem("out_stored")
        raw_loaded = [sem(f"raw_loaded{m}") for m in range(3)]
        vec_loaded, alog_loaded = sem("vec_loaded"), sem("alog_loaded")
        win_loaded, wsk_loaded, wout_loaded = sem("win_loaded"), sem("wsk_loaded"), sem("wout_loaded")
        wd1_loaded, wd2_loaded, wbc_loaded = sem("wd1_loaded"), sem("wd2_loaded"), sem("wbc_loaded")
        abar_zero = sem("abar_zero")
        const_zero, const_ready, dve_const = sem("const_zero"), sem("const_ready"), sem("dve_const")
        abs_ready, asum_ready, asums_ready = sem("abs_ready"), sem("asum_ready"), sem("asums_ready")
        scale_step, gt_ready, q_ready = sem("scale_step"), sem("gt_ready"), sem("q_ready")
        qt_ready, q_saved = sem("qt_ready"), sem("q_saved")
        vec_ready, vcol_ready, vec_step = sem("vec_ready"), sem("vcol_ready"), sem("vec_step")
        a_exp, a_done = sem("a_exp"), sem("a_done")
        pair_ready = [sem(f"pair_ready{p}") for p in range(NPAIR)]
        pair_used = [sem(f"pair_used{p}") for p in range(NPAIR)]
        ub_ready, abar_ready = sem("ub_ready"), sem("abar_ready")
        scanned, hT_ready = sem("scanned"), sem("hT_ready")
        y_added = [sem("y_added0"), sem("y_added1")]
        carry_saved, c_copied = sem("carry_saved"), sem("c_copied")
        ln_stats, ln_moments, xn_ready = sem("ln_stats"), sem("ln_moments"), sem("xn_ready")
        rstd_step, rms_step = sem("rstd_step"), sem("rms_step")
        xr_ready, x12_ready = sem("xr_ready"), sem("x12_ready")
        xh_ready, tanh_ready, silu_ready = sem("xh_ready"), sem("tanh_ready"), sem("silu_ready")
        hh_ready, hl_ready = sem("hh_ready"), sem("hl_ready")
        hist_step, conv_step = sem("hist_step"), sem("conv_step")
        ctanh_ready, xc_ready, xw_ready = sem("ctanh_ready"), sem("xc_ready"), sem("xw_ready")
        sp_step, delta_ready, u_ready = sem("sp_step"), sem("delta_ready"), sem("u_ready")
        gtanh_ready, yx_ready, z_ready = sem("gtanh_ready"), sem("yx_ready"), sem("z_ready")
        pool_go, dve_go = sem("pool_go"), sem("dve_go")
        pe_go, sp_go = sem("pe_go"), sem("sp_go")

        NQ = 6
        QB = 4

        block = ctx.enter_context(nc.Block())

        def phases(eng, run):
            run("fill", -1)
            run("first", 0)
            with eng.Fori(1, NCH - 1) as i:
                run("loop", i)
            run("last", NCH - 1)
            run("drain", NCH)

        def at_slot(names, lag):
            table = {}
            for name in ORDER:
                if name in names:
                    table.setdefault(USE_OF[name] + lag, []).append(name)
            return table

        @block.sync
        def _(sp):
            sp.dma_start(vrow[0:DB, :], norm_w.rearrange("(r p) -> r p", p=P)).then_inc(vec_loaded, 16)
            o = DB
            sp.dma_start(vrow[o:o + TAPS * EB, :], conv_w.rearrange("k o (r p) -> (k o r) p", p=P)).then_inc(vec_loaded, 16)
            o += TAPS * EB
            for v in (conv_b, b_delta_2, W_D):
                sp.dma_start(vrow[o:o + EB, :], v.rearrange("(r p) -> r p", p=P)).then_inc(vec_loaded, 16)
                o += EB
            sp.dma_start(wraw[0][:, :].rearrange("p (f d) -> p f d", d=D),
                         W_up.rearrange("(f p) d -> p f d", p=P)).then_inc(raw_loaded[0], 16)
            sp.dma_start(wraw[1][:, :].rearrange("p (f d) -> p f d", d=D),
                         W_gate.rearrange("(f p) d -> p f d", p=P)).then_inc(raw_loaded[1], 16)
            sp.dma_start(xs[:, 0, :, :], x_dram[0]).then_inc(x_loaded, 16)
            sp.dma_start(wraw[2][:, :].rearrange("p (r f) -> p r f", f=F),
                         W_down.rearrange("(r p) f -> p r f", p=P)).then_inc(raw_loaded[2], 16)
            sp.dma_start(a_neg[:, :, :], A_log.rearrange("(e p) n -> p e n", p=P)).then_inc(alog_loaded, 16)
            sp.dma_start(w_in[:, :, :], W_in.rearrange("(d p) e -> p d e", p=P)).then_inc(win_loaded, 16)
            sp.dma_start(w_d1[:, :, :], W_delta_1.rearrange("(e p) r -> p e r", p=P)).then_inc(wd1_loaded, 16)
            sp.dma_start(w_bc[:, :, 0:N], W_B.rearrange("(e p) n -> p e n", p=P)).then_inc(wbc_loaded, 16)
            sp.dma_start(w_bc[:, :, N:2 * N], W_C.rearrange("(e p) n -> p e n", p=P)).then_inc(wbc_loaded, 16)
            sp.dma_start(w_d2[:, :], W_delta_2).then_inc(wd2_loaded, 16)
            sp.dma_start(w_skip[:, :, :], W_skip.rearrange("(d p) e -> p d e", p=P)).then_inc(wsk_loaded, 16)
            sp.wait_ge(q_saved, NQ * QB)
            sp.dma_start(w_out[:, :, :], W_out.rearrange("(e p) d -> p e d", p=P)).then_inc(wout_loaded, 16)

            def load_x(c):
                sp.wait_ge(x_loaded, 16 * c)
                sp.dma_start(xs[:, bass.ds(c % XSLOTS, 1), :, :].rearrange("p s t d -> p (s t) d"),
                             x_dram[bass.ds(c, 1)].rearrange("s p t d -> p (s t) d")).then_inc(x_loaded, 16)

            def store(ph, i):
                pr, before = job_no(ph, i, "DN2")
                sp.wait_ge(pair_used[pr], before + 1)
                sp.sem_inc(sp_go, 1)
                sp.dma_start(out_dram[bass.ds(i - 1, 1)].rearrange("s p t d -> p (s t) d"),
                             xs[:, bass.ds((i - 1) % XSLOTS, 1), :, :].rearrange("p s t d -> p (s t) d")
                             ).then_inc(out_stored, 16)
                sp.wait_ge(out_stored, 16 * i)
                sp.sem_inc(sp_go, 1)

            def run(ph, i):
                if ph == "fill":
                    load_x(1)
                if ph in ("first", "loop"):
                    if ph == "first":
                        load_x(2)
                    else:
                        sp.wait_ge(x_loaded, 16 * i + 32)
                        sp.sem_inc(sp_go, 1)
                        with_next = i + 2
                        sp.dma_start(xs[:, bass.ds(with_next % XSLOTS, 1), :, :].rearrange("p s t d -> p (s t) d"),
                                     x_dram[bass.ds(with_next % NCH, 1)].rearrange("s p t d -> p (s t) d")
                                     ).then_inc(x_loaded, 16)
                if ph in ("loop", "last", "drain"):
                    store(ph, i)

            phases(sp, run)
            sp.wait_ge(out_stored, 16 * NCH)

        @block.gpsimd
        def _(pool):
            def go():
                pool.sem_inc(pool_go, 1)

            pl = nc.gpsimd
            pl.memset(ident[:, :], 0.0).then_inc(const_zero, 1)
            pl.memset(ident16[:, :], 0.0).then_inc(const_zero, 1)
            pl.memset(ones[:, :], 1.0)
            pl.memset(eps_c[:, :], EPS)
            pl.memset(mhalf_c[:, :], -0.5)
            pl.memset(scale_c[:, :], XN_SCALE)
            pool.wait_ge(const_zero, 2)
            pl.affine_select(out=ident[:, :], in_=ident[:, :], compare_op=ALU.not_equal, fill=1.0, base=0,
                             pattern=[[-1, P]], channel_multiplier=1).then_inc(const_ready, 1)
            pl.affine_select(out=ident16[:, :], in_=ident16[:, :], compare_op=ALU.not_equal, fill=1.0, base=0,
                             pattern=[[-1, P]], channel_multiplier=1).then_inc(const_ready, 1)
            pool.wait_ge(a_exp, 1)
            pl.tensor_scalar(a_neg[:, :, :], a_neg[:, :, :], -1.0, None, ALU.mult).then_inc(a_done, 1)
            pool.wait_ge(vec_step, 2)
            pool.wait_ge(q_saved, NQ * QB)

            pl.memset(abar[:, :, :, 0], 0.0).then_inc(abar_zero, 1)
            pool.wait_ge(dve_const, B + 3)

            def u_times_b(ph, i, s):
                S, half, n = STEPS * i + s, s // N, s % N
                if s % PLANES == 0 and s:
                    pr, before = job_no(ph, i, f"BB_{s // PLANES}")
                    need(pool, pair_used[pr], before + 1)
                if n == 0:
                    u_of(i, half, S)
                    need(pool, u_ready, 2 * i + half + 1)
                used = S - ring_lag(s)
                need(pool, hT_ready, 2 * used + 2)
                if ph != "last" or s < ring_lag(s):
                    need(pool, carry_saved, used + 1)
                go()
                pl.tensor_copy(h[:, s % RING, :, 0], carry[:, HE * s:HE * (s + 1)])
                pl.tensor_tensor(h[:, s % RING, :, 1:], u[:, :, :],
                                 bb[:, (s // PLANES) % 2, s % PLANES:s % PLANES + 1, :].broadcast_to([P, HE, CH]),
                                 ALU.mult).then_inc(ub_ready, 1)

            def planes_0(ph, i):
                pr, before = job_no(ph, i, "BB_0")
                need(pool, pair_used[pr], before + 1)
                go()

            def rstd(ph, i, kind):
                r = rstd_run(ph, i, kind)
                need(pool, ln_moments, TB * ln_run(ph, i, kind) + TB)
                pl.tensor_tensor(rt[:, 0, :], mv[:, :, 1], eps_c[:, :], ALU.add).then_inc(rstd_step, 1)
                need(pool, rstd_step, 3 * r + 1)
                pl.tensor_tensor(rt[:, 1, :], rt[:, 0, :], mhalf_c[:, :], ALU.pow).then_inc(rstd_step, 1)
                need(pool, rstd_step, 3 * r + 2)
                pl.tensor_tensor(rt[:, 2, :], rt[:, 1, :], scale_c[:, :], ALU.mult).then_inc(rstd_step, 1)

            def rms(ph, i):
                k = i + 1
                need(pool, ln_moments, TB * ln_run(ph, i, "p") + TB)
                pl.tensor_tensor(rt[:, 0, :], mv[:, :, 1], eps_c[:, :], ALU.add).then_inc(rms_step, 1)
                need(pool, rms_step, 6 * k + 1)
                pl.tensor_tensor(rt[:, 1, :], rt[:, 0, :], mhalf_c[:, :], ALU.pow).then_inc(rms_step, 1)
                need(pool, rms_step, 6 * k + 2)
                pl.tensor_tensor(rt[:, 3, :], rt[:, 1, :], rt[:, 1, :], ALU.mult).then_inc(rms_step, 1)
                need(pool, rms_step, 6 * k + 3)
                pl.tensor_tensor(rt[:, 4, :], rt[:, 3, :], mv[:, :, 1], ALU.mult).then_inc(rms_step, 1)
                need(pool, rms_step, 6 * k + 4)
                pl.tensor_tensor(rt[:, 3, :], rt[:, 4, :], eps_c[:, :], ALU.add).then_inc(rms_step, 1)
                need(pool, rms_step, 6 * k + 5)
                pl.tensor_tensor(rt[:, 5, :], rt[:, 3, :], mhalf_c[:, :], ALU.pow).then_inc(rms_step, 1)

            def x12(ph, i):
                k = i + 1
                need(pool, xn_ready, TB * ln_run(ph, i, "p") + TB)
                go()
                slot = k % XSLOTS
                pl.tensor_tensor(xs[:, slot, :, :], xs[:, slot, :, :], xn[:, :, :], ALU.add).then_inc(x12_ready, 1)

            def hidden_low(ph, i, kind, p):
                g = PAIRS * ffn_run(ph, i, kind) + p
                need(pool, hh_ready, g + 1)
                pl.tensor_tensor(hl[:, 2 * p:2 * p + 2, :], act[:, p % 2, :].rearrange("q (f t) -> q f t", f=2),
                                 hh[:, 2 * p:2 * p + 2, :], ALU.subtract).then_inc(hl_ready, 1)

            def u_of(c, half, S):
                need(pool, ub_ready, S)
                need(pool, delta_ready, 2 * c + half + 1)
                need(pool, xc_ready, 2 * c + half + 1)
                go()
                pl.tensor_tensor(u[:, :, :], delta[:, half * HE:(half + 1) * HE, :],
                                 xc[:, half * HE:(half + 1) * HE, :], ALU.mult).then_inc(u_ready, 1)

            def x_times_d(i):
                need(pool, z_ready, 2 * i)
                need(pool, xc_ready, 2 * i + 2)
                go()
                pl.tensor_tensor(xw[:, :, :], xc[:, HE:, :], wd[:, HE:].unsqueeze(2).broadcast_to([P, HE, CH]),
                                 ALU.mult).then_inc(xw_ready, 1)

            hl_at = at_slot([f"UG{k}_{p}" for k in (1, 2) for p in range(PAIRS)], 1)

            def run(ph, i):
                has = PHASES[ph]
                scan = "SK_0" in has
                if scan:
                    for s in range(AHEAD):
                        u_times_b(ph, i, s)
                for s in range(STEPS + 2):
                    if scan and s + AHEAD < STEPS:
                        u_times_b(ph, i, s + AHEAD)
                    if s == USE_OF["OM"] and "OM" in has:
                        rstd(ph, i, "2")
                    for name in hl_at.get(s, ()):
                        if name in has:
                            hidden_low(ph, i, int(name[2]), int(name[4]))
                    if s == USE_OF["DN1"] and "DN1" in has:
                        rms(ph, i)
                    if s == USE_OF["DN1"] + 1 and "DN1" in has:
                        x12(ph, i)
                    if s == USE_OF["YT_1"] + 2 and scan:
                        x_times_d(i)
                    if s == NEXT_LN and "T1" in has:
                        rstd(ph, i, "n")
                    if s == USE_OF["BB_0"] + 1 and "BB_0" in has:
                        planes_0(ph, i)

            rstd("fill", -1, "1")
            phases(pool, run)

        @block.scalar
        def _(sc):
            ac = nc.scalar

            junk = ps[:, 0:4, :].rearrange("p a b -> p (a b)")
            for m in range(3):
                sc.wait_ge(raw_loaded[m], 16)
                for q in range(4):
                    if 4 * m + q:
                        sc.wait_ge(abs_ready, 4 * m + q)
                    ac.activation(junk, wraw[m][:, q * F:(q + 1) * F], ACT.Abs,
                                  accum_out=asum[:, m, q:q + 1]).then_inc(abs_ready, 1)
            sc.wait_ge(alog_loaded, 16)
            ac.activation(a_neg[:, :, :], a_neg[:, :, :], ACT.Exp).then_inc(a_exp, 1)

            def save_q(hb):
                m, part = hb // 2, hb % 2
                for b in range(QB):
                    sc.wait_ge(qt_ready, QB * hb + b + 1)
                    src = ps[:, 4 + b, :].bitcast(f16)
                    if m < 2:
                        ac.activation(qT[m][:, b, part * (F // 2):(part + 1) * (F // 2)], src, ACT.Copy,
                                      saturate=False).then_inc(q_saved, 1)
                    else:
                        ac.activation(q_down[:, 4 * b:4 * b + 4, part * (D // 2):(part + 1) * (D // 2)],
                                      src.rearrange("p (f d) -> p f d", f=4), ACT.Copy,
                                      saturate=False).then_inc(q_saved, 1)

            for hb in range(NQ):
                save_q(hb)
            sc.wait_ge(vec_step, 2)
            sc.wait_ge(a_done, 1)
            sc.wait_ge(abar_zero, 1)
            sc.wait_ge(q_saved, NQ * QB)

            def exps(ph, i, s):
                S, half, n = STEPS * i + s, s // N, s % N
                if n == 0:
                    need(sc, delta_ready, 2 * i + half + 1)
                need(sc, scanned, S - ring_lag(s) + 1)
                for e in range(HE):
                    k = half * HE + e
                    ins = ac.activation(abar[:, s % RING, e, 1:], delta[:, k, :], ACT.Exp, scale=a_neg[:, k, n:n + 1])
                ins.then_inc(abar_ready, 1)

            def ready(ph, i, name):
                pr, before = job_no(ph, i, name)
                need(sc, pair_ready[pr], before + 1)
                return pr, pair[pr]

            def flat(pp):
                return pp.rearrange("p a b -> p (a b)")

            def x_high(ph, i, kind):
                pr, pp = ready(ph, i, f"T{kind}")
                ac.activation(xh[:, :, :].rearrange("p d t -> p (d t)"), flat(pp), ACT.Copy).then_inc(xh_ready, 1)

            def tanh_up(ph, i, kind, p):
                g = PAIRS * ffn_run(ph, i, kind) + p
                need(sc, hl_ready, g - 1)
                pr, pp = ready(ph, i, f"UG{kind}_{p}")
                ac.activation(act[:, p % 2, :], pp[:, 0, :], ACT.Tanh, scale=tanh_sc[:, 0:1]).then_inc(tanh_ready, 1)

            def hidden_high(ph, i, kind, p):
                pr, before = job_no(ph, i, f"UG{kind}_{p}")
                need(sc, pair_used[pr], before + 1)
                ac.activation(hh[:, 2 * p:2 * p + 2, :], act[:, p % 2, :].rearrange("q (f t) -> q f t", f=2),
                              ACT.Copy).then_inc(hh_ready, 1)

            def x_norm_T(ph, i):
                pr, pp = ready(ph, i, "Tp")
                for d in range(DB):
                    ins = ac.activation(xrT[:, d, :], flat(pp)[:, d * CH:(d + 1) * CH], ACT.Copy, scale=nw[:, d:d + 1])
                ins.then_inc(pair_used[pr], 1)

            def conv_in(ph, i, half):
                need(sc, conv_step, CONV_STEPS * (2 * (i + 1) + half))
                need(sc, x12_ready, i + 2)
                pr, pp = ready(ph, i, f"IN_{half}")
                ac.activation(cin[:, :, TAPS - 1:], flat(pp).rearrange("p (e t) -> p e t", e=HE), ACT.Copy)
                if half == 0:
                    need(sc, z_ready, 2 * i + 1)
                else:
                    need(sc, xw_ready, i + 1)
                for e in range(HE):
                    b = half * HE + e
                    w = cw[:, (TAPS - 1) * EB + b:(TAPS - 1) * EB + b + 1]
                    ins = ac.activation(xc[:, b, :], flat(pp)[:, e * CH:(e + 1) * CH], ACT.Identity, scale=w, bias=cb[:, b:b + 1])
                ins.then_inc(pair_used[pr], 1)

            def conv_tanh(i, half):
                c = i + 1
                need(sc, conv_step, CONV_STEPS * (2 * c + half + 1))
                need(sc, xc_ready, 2 * c + half)
                ac.activation(tmp_h, xc[:, half * HE:(half + 1) * HE, :], ACT.Tanh).then_inc(ctanh_ready, 1)

            def delta_rank(ph, i):
                pr, pp = ready(ph, i, "D1")
                ac.activation(d1[:, :], pp[:, 0, 0:CH], ACT.Copy).then_inc(pair_used[pr], 1)

            def b_and_c(ph, i):
                need(sc, c_copied, i + 1)
                pr, pp = ready(ph, i, "BC")
                ac.activation(bcn[:, :, :], pp[:, 0, 0:TB * 2 * N].rearrange("p (t n) -> p t n", t=TB),
                              ACT.Copy).then_inc(pair_used[pr], 1)

            def softplus_in(ph, i, half):
                pr, pp = ready(ph, i, f"D2_{half}")
                for e in range(HE):
                    b = half * HE + e
                    ins = ac.activation(delta[:, b, :], flat(pp)[:, e * CH:(e + 1) * CH], ACT.Identity, bias=b2[:, b:b + 1])
                ins.then_inc(pair_used[pr], 1)

            def softplus_log(ph, i, half):
                c = i + 1 if half == 0 else i
                pr, before = job_no(ph, i, f"D2_{half}")
                need(sc, pair_used[pr], before + 1)
                v = delta[:, half * HE:(half + 1) * HE, :]
                ac.activation(tmp_h, v, ACT.Abs).then_inc(sp_step, 1)
                need(sc, sp_step, 3 * (2 * c + half) + 1)
                ac.activation(tmp_h, tmp_h, ACT.Exp, scale=-1.0).then_inc(sp_step, 1)
                need(sc, sp_step, 3 * (2 * c + half) + 2)
                ac.activation(tmp_h, tmp_h, ACT.Ln, bias=1.0).then_inc(sp_step, 1)

            def planes(ph, i, q):
                c = i + 1 if q == 0 else i
                need(sc, ub_ready, STEPS * c + PLANES * (q - 1))
                pr, pp = ready(ph, i, f"BB_{q}")
                ac.activation(bb[:, q % 2, :, :].rearrange("p n t -> p (n t)"), flat(pp), ACT.Copy).then_inc(pair_used[pr], 1)

            def skip_tanh(ph, i, half):
                pr, pp = ready(ph, i, f"SK_{half}")
                ac.activation(gz[:, half * HE:(half + 1) * HE, :].rearrange("p e t -> p (e t)"), flat(pp), ACT.Tanh,
                              scale=0.5).then_inc(gtanh_ready, 1)

            ug = [f"UG{k}_{p}" for k in (1, 2) for p in range(PAIRS)]
            hh_at = at_slot(ug, 1)

            def run(ph, i):
                has = PHASES[ph]
                scan = "SK_0" in has

                def evacuate(name):
                    if name[:2] == "UG":
                        tanh_up(ph, i, int(name[2]), int(name[4]))
                    elif name in ("T1", "T2"):
                        x_high(ph, i, int(name[1]))
                    elif name == "Tp":
                        x_norm_T(ph, i)
                    elif name[:2] == "IN":
                        conv_in(ph, i, int(name[3]))
                    elif name == "D1":
                        delta_rank(ph, i)
                    elif name == "BC":
                        b_and_c(ph, i)
                    elif name[:2] == "SK":
                        skip_tanh(ph, i, int(name[3]))
                    elif name[:2] == "BB":
                        planes(ph, i, int(name[3]))
                    elif name[:2] == "D2":
                        softplus_in(ph, i, int(name[3]))

                if scan:
                    for s in range(AHEAD):
                        exps(ph, i, s)
                for s in range(STEPS + 3):
                    if scan and s + AHEAD < STEPS:
                        exps(ph, i, s + AHEAD)
                    for name in ORDER:
                        if name in has and SLOT_OF[name] == s - 1 and name not in EARLY:
                            evacuate(name)
                    for name in hh_at.get(s, ()):
                        if name in has:
                            hidden_high(ph, i, int(name[2]), int(name[4]))
                    for half in range(2):
                        if f"D2_{half}" in has and s == USE_OF[f"D2_{half}"] + 1:
                            softplus_log(ph, i, half)
                        if f"IN_{half}" in has and s == USE_OF[f"IN_{half}"] + 2:
                            conv_tanh(i, half)
                    for name in ORDER:
                        if name in has and SLOT_OF[name] == s and name in EARLY:
                            evacuate(name)

            phases(sc, run)

        @block.vector
        def _(ve):
            v = nc.vector

            def go():
                ve.sem_inc(dve_go, 1)

            v.memset(keep[:, :], -1).then_inc(dve_const, 1)
            ve.wait_ge(dve_const, 1)
            for b in range(B):
                v.memset(keep[:, b * CPB:b * CPB + 1], 0).then_inc(dve_const, 1)
            v.memset(carry[:, :], 0.0).then_inc(dve_const, 1)
            v.memset(hist[:, :, :, :], 0.0).then_inc(dve_const, 1)
            ve.wait_ge(dve_const, B + 3)

            ve.wait_ge(vec_ready, 1)
            v.tensor_copy(vcol[:, :], ps[:, 7, 0:NV]).then_inc(vcol_ready, 1)
            ve.wait_ge(vcol_ready, 1)
            v.tensor_scalar(vcol[:, DB:DB + (TAPS + 1) * EB], vcol[:, DB:DB + (TAPS + 1) * EB], 0.5, None,
                            ALU.mult).then_inc(vec_step, 1)
            for m in range(3):
                ve.wait_ge(abs_ready, 4 * (m + 1))
                v.reduce_sum(asum1[:, m:m + 1], asum[:, m, :], AX.X).then_inc(asum_ready, 1)
                ve.wait_ge(asums_ready, m + 1)
                v.tensor_scalar(wscale[:, m:m + 1], ps[:, 6, m:m + 1], 1.0 / (F * D), TEPS, ALU.mult,
                                ALU.add).then_inc(scale_step, 1)
                ve.wait_ge(scale_step, 3 * m + 1)
                v.tensor_scalar(thr[:, 0, m:m + 1], wscale[:, m:m + 1], 0.5, None, ALU.mult).then_inc(scale_step, 1)
                v.tensor_scalar(thr[:, 1, m:m + 1], wscale[:, m:m + 1], -0.5, None, ALU.mult).then_inc(scale_step, 1)
                ve.wait_ge(scale_step, 3 * m + 3)
                half_len = F * D // P // 2
                for part in range(2):
                    hb = 2 * m + part
                    if hb >= 2:
                        ve.wait_ge(qt_ready, QB * (hb - 1))
                    src = wraw[m][:, part * half_len:(part + 1) * half_len]
                    v.tensor_scalar(qh[:, hb % 2, :], src, thr[:, 0, m:m + 1], None, ALU.is_gt).then_inc(gt_ready, 1)
                    ve.wait_ge(gt_ready, hb + 1)
                    v.scalar_tensor_tensor(out=qh[:, hb % 2, :], in0=src, scalar=thr[:, 1, m:m + 1],
                                           in1=qh[:, hb % 2, :], op0=ALU.is_lt, op1=ALU.subtract).then_inc(q_ready, 1)
            v.tensor_scalar(tanh_sc[:, :], wscale[:, 0:1], -0.5 / XN_SCALE, None, ALU.mult).then_inc(vec_step, 1)
            v.tensor_tensor(prod_sc[:, 0:1], wscale[:, 0:1], wscale[:, 1:2], ALU.mult).then_inc(scale_step, 1)
            ve.wait_ge(scale_step, 10)
            v.tensor_tensor(prod_sc[:, 1:2], prod_sc[:, 0:1], wscale[:, 2:3], ALU.mult).then_inc(scale_step, 1)
            ve.wait_ge(scale_step, 11)
            v.tensor_scalar(down_sc[:, :], prod_sc[:, 1:2], -0.5 * 0.5 / (HID_SCALE * XN_SCALE * XN_SCALE), None,
                            ALU.mult).then_inc(scale_step, 1)
            ve.wait_ge(scale_step, 12)
            ve.wait_ge(a_done, 1)
            ve.wait_ge(q_saved, NQ * QB)

            def ready(ph, i, name):
                pr, before = job_no(ph, i, name)
                need(ve, pair_ready[pr], before + 1)
                return pr, pair[pr]

            def flat(pp):
                return pp.rearrange("p a b -> p (a b)")

            def start_chunk(i):
                need(ve, delta_ready, 2 * i + 1)
                for t in range(TB):
                    need(ve, y_added[t], STEPS * i)
                go()
                v.tensor_copy(ccur[:, :, :], bcn[:, :, N:2 * N]).then_inc(c_copied, 1)

            def scan_of(i, s):
                S = STEPS * i + s
                need(ve, abar_ready, S + 1)
                need(ve, ub_ready, S + 1)
                hh_s = h[:, s % RING, :, :].rearrange("p e t -> p (e t)")
                v.tensor_tensor_scan(hh_s, abar[:, s % RING, :, :].rearrange("p e t -> p (e t)"), hh_s, 0.0, ALU.mult,
                                     ALU.add).then_inc(scanned, 1)

            def save_carry(i, s):
                need(ve, scanned, STEPS * i + s + 1)
                nxt = keep[:, i + 1:i + 2] if isinstance(i, int) else keep[:, bass.ds(i + 1, 1)]
                v.tensor_tensor(carry[:, HE * s:HE * (s + 1)].bitcast(i32), h[:, s % RING, :, CH].bitcast(i32),
                                nxt.broadcast_to([P, HE]), ALU.bitwise_and).then_inc(carry_saved, 1)

            def y_add(ph, i, s):
                S, half, n = STEPS * i + s, s // N, s % N
                if s == 0:
                    need(ve, c_copied, i + 1)
                if n == 0 and (half == 1 or ph == "loop" or ph == "last"):
                    pr, before = job_no(ph, i, f"YT_{1 - half}")
                    need(ve, pair_ready[pr], before + 1)
                for t in range(TB):
                    need(ve, hT_ready, 2 * S + t + 1)
                    yy = y[:, t, :]
                    cc = ccur[:, t, n:n + 1]
                    if n == 0:
                        ins = v.tensor_scalar(yy, hT[:, t, :], cc, None, ALU.mult)
                    else:
                        need(ve, y_added[t], S)
                        ins = v.scalar_tensor_tensor(out=yy, in0=hT[:, t, :], scalar=cc, in1=yy, op0=ALU.mult, op1=ALU.add)
                    ins.then_inc(y_added[t], 1)

            def moments(ph, i, kind, slot):
                l = ln_run(ph, i, kind)
                go()
                for t in range(TB):
                    v.bn_stats(st[:, t, :], xs[:, slot, t, :]).then_inc(ln_stats, 1)
                need(ve, ln_stats, TB * l + TB)
                go()
                for t in range(TB):
                    v.bn_aggr(mv[:, t, :], st[:, t, :]).then_inc(ln_moments, 1)

            def normalise(ph, i, kind, slot):
                row = 2
                if kind == "p":
                    row = 1
                    need(ve, rms_step, 6 * (i + 1) + 6)
                else:
                    need(ve, rstd_step, 3 * rstd_run(ph, i, kind) + 3)
                l = ln_run(ph, i, kind)
                for t in range(TB):
                    v.tensor_scalar(xn[:, t, :], xs[:, slot, t, :], mv[:, t, 0:1], rt[:, row, t:t + 1], ALU.subtract,
                                    ALU.mult).then_inc(xn_ready, 1)

            def rms_scaled(ph, i):
                need(ve, xn_ready, TB * ln_run(ph, i, "p") + TB)
                for t in range(TB):
                    ins = v.tensor_scalar(xr[:, t, :], xn[:, t, :], rt[:, 5, t:t + 1], None, ALU.mult)
                ins.then_inc(xr_ready, 1)

            def x_low(ph, i, kind):
                need(ve, xh_ready, ffn_run(ph, i, kind) + 1)
                pr, pp = ready(ph, i, f"T{kind}")
                v.tensor_tensor(xl[:, :, :].rearrange("p d t -> p (d t)"), flat(pp), xh[:, :, :].rearrange("p d t -> p (d t)"),
                                ALU.subtract).then_inc(pair_used[pr], 1)

            def hidden(ph, i, kind, p):
                g = PAIRS * ffn_run(ph, i, kind) + p
                need(ve, tanh_ready, g + 1)
                pr, pp = ready(ph, i, f"UG{kind}_{p}")
                a = act[:, p % 2, :]
                v.scalar_tensor_tensor(out=a, in0=a, scalar=1.0, in1=pp[:, 0, :], op0=ALU.add, op1=ALU.mult).then_inc(silu_ready, 1)
                need(ve, silu_ready, g + 1)
                v.scalar_tensor_tensor(out=a, in0=pp[:, 1, :], scalar=HID_SCALE, in1=a, op0=ALU.mult,
                                       op1=ALU.mult).then_inc(pair_used[pr], 1)

            def add_to_stream(ph, i, name, slot, factor):
                pr, pp = ready(ph, i, name)
                for t in range(TB):
                    xx = xs[:, slot, t, :]
                    ins = v.scalar_tensor_tensor(out=xx, in0=pp[:, t, :], scalar=factor, in1=xx, op0=ALU.mult, op1=ALU.add)
                ins.then_inc(pair_used[pr], 1)
                need(ve, pair_used[pr], job_no(ph, i, name)[1] + 1)

            def conv(ph, i, half, part):
                c = i + 1
                g = CONV_STEPS * (2 * c + half)
                pr, before = job_no(ph, i, f"IN_{half}")
                if part == 0:
                    need(ve, conv_step, g)
                    need(ve, x12_ready, c + 1)
                    pt, tb = job_no(ph, i, "Tp")
                    need(ve, pair_ready[pt], tb + 1)
                    v.tensor_tensor(cin[:, :, 0:TAPS - 1].bitcast(i32), hist[:, half, :, :].bitcast(i32),
                                    (keep[:, c:c + 1] if isinstance(c, int) else keep[:, bass.ds(c, 1)])
                                    .unsqueeze(2).broadcast_to([P, HE, TAPS - 1]), ALU.bitwise_and).then_inc(conv_step, 1)
                    need(ve, pair_used[pr], before + 1)
                    need(ve, conv_step, g + 1)
                    v.tensor_copy(hist[:, half, :, :], cin[:, :, CH:CH + TAPS - 1]).then_inc(conv_step, 1)
                g += 2 + part * (TAPS - 1) * HE // 2
                for tap in range(TAPS - 1):
                    for e in range(HE // 2):
                        b = half * HE + part * HE // 2 + e
                        if tap:
                            need(ve, conv_step, g + HE // 2 * (tap - 1) + e + 1)
                        v.scalar_tensor_tensor(out=xc[:, b, :], in0=cin[:, part * HE // 2 + e, tap:tap + CH],
                                               scalar=cw[:, tap * EB + b:tap * EB + b + 1], in1=xc[:, b, :], op0=ALU.mult,
                                               op1=ALU.add).then_inc(conv_step, 1)

            def conv_silu(i, half):
                c = i + 1
                need(ve, ctanh_ready, 2 * c + half + 1)
                xx = xc[:, half * HE:(half + 1) * HE, :]
                v.scalar_tensor_tensor(out=xx, in0=tmp_h, scalar=1.0, in1=xx, op0=ALU.add, op1=ALU.mult).then_inc(xc_ready, 1)

            def softplus(c, half):
                need(ve, sp_step, 3 * (2 * c + half) + 3)
                dd = delta[:, half * HE:(half + 1) * HE, :]
                v.scalar_tensor_tensor(out=dd, in0=dd, scalar=0.0, in1=tmp_h, op0=ALU.max, op1=ALU.add).then_inc(delta_ready, 1)

            def skip_gate(ph, i, half):
                need(ve, gtanh_ready, 2 * i + half + 1)
                pr, pp = ready(ph, i, f"SK_{half}")
                gg = gz[:, half * HE:(half + 1) * HE, :].rearrange("p e t -> p (e t)")
                v.scalar_tensor_tensor(out=gg, in0=gg, scalar=1.0, in1=flat(pp), op0=ALU.add, op1=ALU.mult).then_inc(pair_used[pr], 1)

            def gated(ph, i, half):
                c = i if half == 0 else i - 1
                pr, pp = ready(ph, i, f"YT_{half}")
                hb = slice(half * HE, (half + 1) * HE)
                if half == 0:
                    yx = xc[:, hb, :]
                    for e in range(HE):
                        ins = v.scalar_tensor_tensor(out=yx[:, e, :], in0=yx[:, e, :], scalar=wd[:, e:e + 1],
                                                     in1=flat(pp)[:, e * CH:(e + 1) * CH], op0=ALU.mult, op1=ALU.add)
                else:
                    need(ve, xw_ready, i)
                    yx = xw[:, :, :]
                    ins = v.tensor_tensor(yx.rearrange("p e t -> p (e t)"), flat(pp), yx.rearrange("p e t -> p (e t)"), ALU.add)
                ins.then_inc(pair_used[pr], 1)
                need(ve, pair_used[pr], job_no(ph, i, f"YT_{half}")[1] + 1)
                v.tensor_tensor(gz[:, hb, :], yx, gz[:, hb, :], ALU.mult).then_inc(z_ready, 1)

            def run(ph, i):
                scan = "SK_0" in PHASES[ph]
                if scan:
                    start_chunk(i)
                    scan_of(i, 0)
                for s in range(STEPS + 3):
                    if scan and s + 1 < STEPS:
                        scan_of(i, s + 1)
                    if scan and s < STEPS and ph != "last":
                        save_carry(i, s)
                    for name in ORDER:
                        if name in PHASES[ph] and SLOT_OF[name] == s - 1 and name not in EARLY:
                            use(ph, i, name)
                    if scan and 1 <= s <= STEPS:
                        y_add(ph, i, s - 1)
                    background(ph, i, s)
                    for name in ORDER:
                        if name in PHASES[ph] and SLOT_OF[name] == s and name in EARLY:
                            use(ph, i, name)

            def use(ph, i, name):
                nslot = (i + 1) % XSLOTS
                pslot = (i - 1) % XSLOTS
                if name[:2] == "UG":
                    hidden(ph, i, int(name[2]), int(name[4]))
                elif name in ("T1", "T2"):
                    x_low(ph, i, int(name[1]))
                elif name == "OM":
                    add_to_stream(ph, i, "OM", pslot, 0.5)
                    moments(ph, i, "2", pslot)
                elif name == "DN1":
                    add_to_stream(ph, i, "DN1", nslot, down_sc[:, 0:1])
                    moments(ph, i, "p", nslot)
                elif name == "DN2":
                    add_to_stream(ph, i, "DN2", pslot, down_sc[:, 0:1])
                elif name[:2] == "SK":
                    skip_gate(ph, i, int(name[3]))
                elif name[:2] == "YT":
                    gated(ph, i, int(name[3]))

            def background(ph, i, s):
                has = PHASES[ph]
                nslot = (i + 1) % XSLOTS
                pslot = (i - 1) % XSLOTS

                def after(name, lag):
                    return name in has and s == USE_OF[name] + lag

                for half in range(2):
                    if after(f"IN_{half}", 0):
                        conv(ph, i, half, 0)
                    if after(f"IN_{half}", 1):
                        conv(ph, i, half, 1)
                    if after(f"IN_{half}", 2):
                        conv_silu(i, half)
                    if after(f"D2_{half}", 1):
                        softplus(i + 1 if half == 0 else i, half)
                if after("OM", 1):
                    if "Tp" in has:
                        need(ve, x12_ready, i + 1)
                    normalise(ph, i, "2", pslot)
                if after("DN1", 1):
                    if "T2" in has:
                        pr, before = job_no(ph, i, "T2")
                        need(ve, pair_ready[pr], before + 1)
                    normalise(ph, i, "p", nslot)
                    rms_scaled(ph, i)
                if "T1" in has and s == NEXT_LN:
                    need(ve, x_loaded, 16 * (i + 3))
                    moments(ph, i, "n", (i + 2) % XSLOTS)
                if "T1" in has and s == NEXT_LN + 1:
                    need(ve, conv_step, CONV_STEPS * (2 * i + 4))
                    normalise(ph, i, "n", (i + 2) % XSLOTS)

            ve.wait_ge(x_loaded, 16)
            moments("fill", -1, "1", 0)
            normalise("fill", -1, "1", 0)
            phases(ve, run)

        @block.tensor
        def _(pe):
            te = nc.tensor

            pe.wait_ge(const_ready, 2)
            pe.wait_ge(vec_loaded, 16 * 5)
            te.transpose(ps[:, 7, 0:NV], vrow[:, :], ident[0:NV, 0:NV]).then_inc(vec_ready, 1)
            pe.wait_ge(vcol_ready, 1)
            for m in range(3):
                pe.wait_ge(asum_ready, m + 1)
                if m:
                    pe.wait_ge(q_saved, QB * 2 * m)
                te.matmul(ps[:, 6, m:m + 1], ones[:, :], asum1[:, m:m + 1], start=True, stop=True).then_inc(asums_ready, 1)
                for part in range(2):
                    hb = 2 * m + part
                    pe.wait_ge(q_ready, hb + 1)
                    if hb:
                        pe.wait_ge(q_saved, QB * hb)
                    src = qh[:, hb % 2, :]
                    for b in range(QB):
                        bank = ps[:, 4 + b, :].bitcast(f16)
                        for j in range(8):
                            if m < 2:
                                blk = src[:, j * D + b * P:j * D + (b + 1) * P]
                            else:
                                f, d = 4 * b + j // 2, j % 2
                                blk = src[:, d * F + f * P:d * F + (f + 1) * P]
                            ins = te.transpose(bank[:, j * P:(j + 1) * P], blk, ident16[:, :])
                        ins.then_inc(qt_ready, 1)
            pe.wait_ge(q_saved, NQ * QB)
            for sm, n in ((win_loaded, 1), (wd1_loaded, 1), (wbc_loaded, 2), (wd2_loaded, 1), (wsk_loaded, 1), (wout_loaded, 1)):
                pe.wait_ge(sm, 16 * n)

            def states_T(i, s):
                S = STEPS * i + s
                need(pe, scanned, S + 1)
                for t in range(TB):
                    need(pe, y_added[t], S)
                    for e in range(HE):
                        ins = te.transpose(hT[:, t, e * P:(e + 1) * P], h[:, s % RING, e, 1 + t * P:1 + (t + 1) * P], ident[:, :])
                    ins.then_inc(hT_ready, 1)

            def opened(ph, i, name, lo=0):
                pr, before = job_no(ph, i, name)
                if lo == 0:
                    need(pe, pair_used[pr], before)
                return pr, pair[pr]

            def flat(pp):
                return pp.rearrange("p a b -> p (a b)")

            def used(ph, i, name):
                pr, before = job_no(ph, i, name)
                need(pe, pair_used[pr], before + 1)

            def rows_T(ph, i, name, src):
                pr, pp = opened(ph, i, name)
                for d in range(DB):
                    for t in range(TB):
                        ins = te.transpose(flat(pp)[:, d * CH + t * P:d * CH + (t + 1) * P], src[:, t, d * P:(d + 1) * P],
                                           ident[:, :])
                ins.then_inc(pair_ready[pr], 1)

            def up_gate(ph, i, kind, p):
                name = f"UG{kind}_{p}"
                pr, pp = opened(ph, i, name)
                if p == 0:
                    used(ph, i, f"T{kind}")
                pe.sem_inc(pe_go, 1)
                for b, w in enumerate((q_up, q_gate)):
                    for f in range(2):
                        col = (2 * p + f) * P
                        for d in range(DB):
                            for part in (xh, xl):
                                ins = te.matmul(pp[:, b, f * CH:(f + 1) * CH], w[:, d, col:col + P], part[:, d, :],
                                                start=(d == 0 and part is xh), stop=(d == DB - 1 and part is xl))
                ins.then_inc(pair_ready[pr], 1)

            def down(ph, i, kind, lo, hi):
                name = f"DN{kind}"
                pr, pp = opened(ph, i, name, lo)
                need(pe, hl_ready, PAIRS * ffn_run(ph, i, kind) + (hi + 1) // 2)
                pe.sem_inc(pe_go, 1)
                for t in range(TB):
                    for f in range(lo, hi):
                        for part in (hh, hl):
                            ins = te.matmul(pp[:, t, :], part[:, f, t * P:(t + 1) * P], q_down[:, f, :],
                                            start=(f == 0 and part is hh), stop=(f == FB - 1 and part is hl))
                if hi == FB:
                    ins.then_inc(pair_ready[pr], 1)

            def project(ph, i, name, w, lo, hi):
                half = int(name[3])
                pr, pp = opened(ph, i, name, lo)
                for e in range(lo, hi):
                    col = (half * HE + e) * P
                    for d in range(DB):
                        ins = te.matmul(flat(pp)[:, e * CH:(e + 1) * CH], w[:, d, col:col + P], xrT[:, d, :],
                                        start=(d == 0), stop=(d == DB - 1))
                if hi == HE:
                    ins.then_inc(pair_ready[pr], 1)

            def delta_1(ph, i):
                need(pe, xc_ready, 2 * (i + 1) + 2)
                pr, pp = opened(ph, i, "D1")
                for e in range(EB):
                    ins = te.matmul(pp[:, 0, 0:CH], w_d1[:, e, :], xc[:, e, :], start=(e == 0), stop=(e == EB - 1))
                ins.then_inc(pair_ready[pr], 1)

            def b_and_c(ph, i):
                pr, pp = opened(ph, i, "BC")
                for t in range(TB):
                    for e in range(EB):
                        ins = te.matmul(pp[:, 0, t * 2 * N:(t + 1) * 2 * N], xc[:, e, t * P:(t + 1) * P], w_bc[:, e, :],
                                        start=(e == 0), stop=(e == EB - 1))
                ins.then_inc(pair_ready[pr], 1)

            def delta_2(ph, i, half):
                pr, pp = opened(ph, i, f"D2_{half}")
                if half == 0:
                    used(ph, i, "D1")
                for e in range(HE):
                    col = (half * HE + e) * P
                    ins = te.matmul(flat(pp)[:, e * CH:(e + 1) * CH], w_d2[:, col:col + P], d1[:, :], start=True, stop=True)
                ins.then_inc(pair_ready[pr], 1)

            def b_planes(ph, i, q):
                if q == 0:
                    used(ph, i, "BC")
                pr, pp = opened(ph, i, f"BB_{q}")
                for j in range(PLANES):
                    n = (PLANES * q + j) % N
                    for t in range(TB):
                        ins = te.transpose(flat(pp)[:, j * CH + t * P:j * CH + (t + 1) * P],
                                           bcn[:, t, n:n + 1].broadcast_to([P, P]), ident[:, :])
                ins.then_inc(pair_ready[pr], 1)

            def y_T(ph, i, half):
                c = i if half == 0 else i - 1
                for t in range(TB):
                    need(pe, y_added[t], STEPS * c + N * (half + 1))
                pr, pp = opened(ph, i, f"YT_{half}")
                for e in range(HE):
                    for t in range(TB):
                        ins = te.transpose(flat(pp)[:, e * CH + t * P:e * CH + (t + 1) * P], y[:, t, e * P:(e + 1) * P],
                                           ident[:, :])
                ins.then_inc(pair_ready[pr], 1)

            def out_proj(ph, i, lo, hi):
                pr, pp = opened(ph, i, "OM", lo)
                if lo == 0 or hi > HE:
                    need(pe, z_ready, 2 * i - 1 if hi <= HE else 2 * i)
                for t in range(TB):
                    for e in range(lo, hi):
                        ins = te.matmul(pp[:, t, :], gz[:, e, t * P:(t + 1) * P], w_out[:, e, :],
                                        start=(e == 0), stop=(e == EB - 1))
                if hi == EB:
                    ins.then_inc(pair_ready[pr], 1)

            def job(ph, i, name, lo, hi):
                if name[:2] == "UG":
                    up_gate(ph, i, int(name[2]), int(name[4]))
                elif name[:2] == "DN":
                    down(ph, i, int(name[2]), lo, hi)
                elif name in ("T1", "T2"):
                    need(pe, xn_ready, TB * ln_run(ph, i, name[1]) + TB)
                    rows_T(ph, i, name, xn)
                elif name == "Tp":
                    need(pe, xr_ready, i + 2)
                    rows_T(ph, i, name, xr)
                elif name[:2] == "IN":
                    if lo == 0:
                        used(ph, i, "Tp")
                    project(ph, i, name, w_in, lo, hi)
                elif name[:2] == "SK":
                    project(ph, i, name, w_skip, lo, hi)
                elif name == "D1":
                    delta_1(ph, i)
                elif name == "BC":
                    b_and_c(ph, i)
                elif name[:2] == "D2":
                    delta_2(ph, i, int(name[3]))
                elif name[:2] == "BB":
                    b_planes(ph, i, int(name[3]))
                elif name[:2] == "YT":
                    y_T(ph, i, int(name[3]))
                else:
                    out_proj(ph, i, lo, hi)

            def run(ph, i):
                has = PHASES[ph]
                scan = "SK_0" in has
                for s in range(STEPS):
                    for name, lo, hi in SLOTS[s]:
                        if name in has:
                            job(ph, i, name, lo, hi)
                    if scan:
                        states_T(i, s)

            phases(pe, run)


_ORDER = ['resid', 'norm_w', 'W_skip', 'W_in', 'conv_w', 'conv_b', 'W_delta_1', 'W_delta_2', 'b_delta_2', 'W_B', 'W_C',
          'A_log', 'W_D', 'W_out']
_INS = [f'L0_attn_{n}' for n in _ORDER] + ['L0_ffn_W_up', 'L0_ffn_W_gate', 'L0_ffn_W_down']


def kernel(**inputs):
    import numpy as _np
    import concourse.bacc as _bacc
    from concourse import mybir as _mybir
    from concourse.bass_utils import run_bass_kernel_spmd as _run

    nc = _bacc.Bacc("TRN2", target_bir_lowering=False, num_devices=1)
    arrays, args = {}, []
    for name in _INS:
        a = _np.ascontiguousarray(inputs[name])
        arrays[f"in_{name}_dram"] = a
        args.append(nc.dram_tensor(f"in_{name}_dram", a.shape, _mybir.dt.from_np(a.dtype), kind="ExternalInput").ap())
    o = nc.dram_tensor("out_dram", (B, L, D), _mybir.dt.float32, kind="ExternalOutput").ap()
    macaron_kernel(nc, *args, o)
    r = _run(nc, [arrays], core_ids=[0])
    return r.results[0]["out_dram"]
```

```python
import numpy as np

import concourse.bass as bass
from concourse import mybir
from contextlib import ExitStack

P = 128
D, E, F, N, DD = 512, 1024, 2048, 16, 128
B, L = 4, 1024
TAPS = 4
TOK = B * L
CH = 256
TB = CH // P
NCH = TOK // CH
CPB = L // CH
DB, EB, FB = D // P, E // P, F // P
HE = EB // 2
CONV_STEPS = 2 + (TAPS - 1) * HE
STEPS = 2 * N
PAIRS = FB // 2
XSLOTS = 4
EPS = 1e-5
TEPS = 1e-8
QUARTERS = 4
XN_SCALE = 1024.0
HID_SCALE = 2.0 ** -24

PARTS = {"OM": EB, "DN1": FB, "DN2": FB, "SK_0": HE, "SK_1": HE, "IN_0": HE, "IN_1": HE}
PLANES = 4
LOADS = 6


def state_of(s):
    return s if s < N else (s + N // 2) % N


def planes_of(s):
    q = s // PLANES
    return q if s < N else q - 2


LOOP_SLOTS = [
    ["D2_1", "T1", ("OM", 0, 1)],
    ["YT_1", ("OM", 1, 3)],
    [("OM", 3, 4), "UG1_0"],
    [("OM", 4, 7)],
    [("OM", 7, 8), "UG1_1"],
    ["UG1_2"],
    ["UG1_3", ("SK_0", 0, 2)],
    ["UG1_4"],
    ["UG1_5", ("SK_0", 2, 3)],
    ["UG1_6"],
    ["UG1_7", ("SK_0", 3, 4)],
    [("DN1", 0, 6)],
    ["T2", ("DN1", 6, 11)],
    [("DN1", 11, 16)],
    ["UG2_0", ("SK_1", 0, 2)],
    [("SK_1", 2, 4), "UG2_1"],
    ["Tp", "UG2_2"],
    ["YT_0", ("IN_0", 0, 2)],
    [("IN_0", 2, 4)],
    ["UG2_3"],
    [("IN_1", 0, 3)],
    ["UG2_4", ("IN_1", 3, 4)],
    [("DN2", 0, 4)],
    [("DN2", 4, 8)],
    ["UG2_5"],
    ["D1", "BC"],
    ["BT", "UG2_6"],
    ["UG2_7"],
    ["D2_0", ("DN2", 8, 10)],
    [("DN2", 10, 12)],
    [("DN2", 12, 14)],
    [("DN2", 14, 16)],
]
FIRST_SLOTS = [
    ["D2_1", "T1"],
    [("SK_0", 0, 1)],
    ["UG1_0"],
    ["UG1_1"],
    ["UG1_2"],
    ["UG1_3"],
    ["UG1_4"],
    ["UG1_5"],
    ["UG1_6"],
    ["UG1_7"],
    [("DN1", 0, 4)],
    [("DN1", 4, 8)],
    [("DN1", 8, 12)],
    [("DN1", 12, 16)],
    [("SK_0", 1, 3)],
    [("SK_0", 3, 4)],
    [("SK_1", 0, 4)],
    ["Tp", "YT_0"],
    [("IN_0", 0, 2)],
    [("IN_0", 2, 4)],
    [("IN_1", 0, 2)],
    [("IN_1", 2, 4)],
    [],
    [],
    [],
    ["D1", "BC"],
    ["BT"],
    ["D2_0"],
    [],
    [],
    [],
    [],
]
LAST_SLOTS = [
    ["D2_1", ("OM", 0, 1)],
    ["YT_1", ("OM", 1, 2)],
    [("OM", 2, 4)],
    [("OM", 4, 6)],
    [("OM", 6, 8)],
    [("SK_0", 0, 2)],
    [("SK_0", 2, 4)],
    ["T2", ("SK_1", 0, 1)],
    ["UG2_0"],
    [("SK_1", 1, 2)],
    ["UG2_1"],
    [("SK_1", 2, 4)],
    ["UG2_2"],
    [("DN2", 0, 2)],
    ["UG2_3"],
    [("DN2", 2, 4)],
    ["UG2_4"],
    ["YT_0"],
    ["UG2_5"],
    [("DN2", 4, 6)],
    ["UG2_6"],
    [("DN2", 6, 8)],
    ["UG2_7"],
    [("DN2", 8, 10)],
    [("DN2", 10, 12)],
    [("DN2", 12, 14)],
    [("DN2", 14, 16)],
    [],
    [],
    [],
    [],
    [],
]
PREV = {"YT_1", "OM", "T2", "DN2"} | {f"UG2_{p}" for p in range(PAIRS)}
THIS = {"D2_1", "SK_0", "SK_1", "YT_0"}
NEXT = {"T1", "DN1", "Tp", "IN_0", "IN_1", "D1", "BC", "BT", "D2_0"} | {f"UG1_{p}" for p in range(PAIRS)}
PHASES = {"fill": NEXT, "first": THIS | NEXT, "loop": PREV | THIS | NEXT, "last": PREV | THIS, "drain": PREV}
PLAN = {"fill": LOOP_SLOTS, "first": FIRST_SLOTS, "loop": LOOP_SLOTS, "last": LAST_SLOTS, "drain": LOOP_SLOTS}
SLOTS, ORDER = {}, {}
SLOT_OF = {}
EARLY = {}
USE_OF = {}
for _ph, _has in PHASES.items():
    _all = [[j if isinstance(j, tuple) else (j, 0, 1) for j in jobs] for jobs in PLAN[_ph]]
    SLOTS[_ph] = [[j for j in jobs if j[0] in _has] for jobs in _all]
    ORDER[_ph] = [n for jobs in SLOTS[_ph] for n, lo, hi in jobs if lo == 0]
    SLOT_OF[_ph] = {n: s for s, jobs in enumerate(SLOTS[_ph]) for n, lo, hi in jobs if hi == PARTS.get(n, 1)}
    EARLY[_ph] = {n for jobs in SLOTS[_ph] for n, lo, hi in jobs[:-1] if hi == PARTS.get(n, 1)}
    USE_OF[_ph] = {n: s + (n not in EARLY[_ph]) for n, s in SLOT_OF[_ph].items()}
    assert set(ORDER[_ph]) == _has and len(SLOTS[_ph]) == STEPS
NPAIR = 3
XD_SLOT = 4
NEXT_LN = 26
AHEAD = 2
RING = 3


BEFORE = [("T1", "UG1_0"), ("T2", "UG2_0"), ("UG1_7", "T2"), ("UG1_7", "DN1 end"), ("DN1 end", "UG2_0"), ("OM end", "SK_0"),
          ("OM end", "SK_1"), ("SK_0 end", "YT_0"), ("SK_0 end", "Tp"), ("SK_1 end", "Tp"), ("Tp", "IN_0"),
          ("IN_0 end", "IN_1"), ("IN_1 end", "D1"), ("D2_1", "D1"), ("D1", "BC"), ("BC", "BT"), ("D1", "D2_0")]
BEFORE += [(f"UG{k}_{p}", f"UG{k}_{p + 1}") for k in (1, 2) for p in range(PAIRS - 1)]
for _ph in PHASES:
    _pos = {}
    for _name, _lo, _hi in (j for jobs in SLOTS[_ph] for j in jobs):
        _pos.setdefault(_name, len(_pos))
        if _hi == PARTS.get(_name):
            _pos[_name + " end"] = len(_pos)
    for _a, _b in BEFORE:
        assert _a not in _pos or _b not in _pos or _pos[_a] < _pos[_b], (_ph, _a, _b)


def after(ph, name, lag, s):
    return name in PHASES[ph] and s == USE_OF[ph][name] + lag


def results(ph, s, late):
    return [n for n in ORDER[ph] if USE_OF[ph][n] == s and (n in EARLY[ph]) == late and (ph, n) != ("fill", "T1")]


def pairs_of(ph, end):
    pair, owner, end, k = {}, [None] * NPAIR, [e - max(end) - 1 for e in end], 0
    for pieces in SLOTS[ph]:
        for name, lo, hi in pieces:
            k += 1
            if lo == 0:
                p = min((p for p in range(NPAIR) if owner[p] is None), key=lambda p: end[p])
                pair[name], owner[p] = p, name
            if hi == PARTS.get(name, 1):
                owner[pair[name]], end[pair[name]] = None, k
    return pair, end


def planes_loaded(c, q):
    return LOADS // 2 * c + q // 2 + 1


PAIR_OF = {}
_end = list(range(NPAIR))
for _ph in PHASES:
    if _ph == "loop":
        _, _end = pairs_of(_ph, _end)
    PAIR_OF[_ph], _end = pairs_of(_ph, _end)
JOBS = {(ph, p): [n for n in ORDER[ph] if PAIR_OF[ph][n] == p] for ph in PHASES for p in range(NPAIR)}


def job_no(ph, i, name):
    p = PAIR_OF[ph][name]
    size = {f: len(JOBS[f, p]) for f in PHASES}
    before = JOBS[ph, p].index(name)
    if ph != "fill":
        before += size["fill"]
    if ph == "loop":
        before = before + size["first"] - size["loop"] + size["loop"] * i
    elif ph in ("last", "drain"):
        before += size["first"] + size["loop"] * (NCH - 2) + (size["last"] if ph == "drain" else 0)
    return p, before


def ring_lag(s):
    return RING if s >= STEPS % RING else STEPS % RING


def ffn_run(ph, i, kind):
    if ph == "fill":
        return 0
    if ph == "first":
        return 1
    return 2 * i + (kind - 1) if ph == "loop" else (2 * NCH - 2 if ph == "last" else 2 * NCH - 1)


def ln_run(ph, i, kind):
    if ph in ("fill", "first"):
        return {"fill": 0, "first": 2}[ph] + {"1": 0, "p": 1, "n": 2}[kind]
    if ph == "loop":
        return 3 * i + {"1": 1, "2": 2, "p": 3, "n": 4}[kind]
    return 3 * NCH - 1 + (0 if ph == "last" else 1)


def rstd_run(ph, i, kind):
    if ph in ("fill", "first"):
        return {"fill": 0, "first": 1}[ph] + {"1": 0, "n": 1}[kind]
    if ph == "loop":
        return 2 * i + {"1": 0, "2": 1, "n": 2}[kind]
    return 2 * NCH - 1 + (0 if ph == "last" else 1)


def need(eng, sem, value):
    if isinstance(value, int) and value <= 0:
        return
    eng.wait_ge(sem, value)


def macaron_kernel(nc, resid, norm_w, W_skip, W_in, conv_w, conv_b, W_delta_1, W_delta_2, b_delta_2, W_B, W_C,
                   A_log, W_D, W_out, W_up, W_gate, W_down, out, b_dram):
    f32, f16, f8, i32 = mybir.dt.float32, mybir.dt.float16, mybir.dt.float8e4, mybir.dt.int32
    ACT = mybir.ActivationFunctionType
    ALU = mybir.AluOpType
    AX = mybir.AxisListType

    x_dram = resid.rearrange("b l d -> (b l) d").rearrange("(c t p) d -> c p t d", t=TB, p=P)
    out_dram = out.rearrange("b l d -> (b l) d").rearrange("(c t p) d -> c p t d", t=TB, p=P)

    ctx = ExitStack()
    with ctx:
        def sb(name, shape, dt=f32, where=ctx):
            return where.enter_context(nc.sbuf_tensor(name, shape, dt))

        def sem(name):
            return ctx.enter_context(nc.semaphore(name))

        qT = [sb("q_up", [P, DB, F], f8), sb("q_gate", [P, DB, F], f8), sb("q_down", [P, FB, D], f8)]
        q_up, q_gate, q_down = qT
        w_in = sb("w_in", [P, DB, E])
        w_skip = sb("w_skip", [P, DB, E])
        w_out = sb("w_out", [P, EB, D])
        w_d1 = sb("w_d1", [P, EB, DD])
        w_d2 = sb("w_d2", [P, E])
        w_bc = sb("w_bc", [P, EB, 2 * N])
        a_neg = sb("a_neg", [P, EB, N])
        NV = DB + TAPS * EB + 3 * EB
        vrow = sb("vrow", [NV, P])
        vcol = sb("vcol", [P, NV])
        nw = vcol[:, 0:DB]
        cw = vcol[:, DB:DB + TAPS * EB]
        cb = vcol[:, DB + TAPS * EB:DB + (TAPS + 1) * EB]
        b2 = vcol[:, DB + (TAPS + 1) * EB:DB + (TAPS + 2) * EB]
        wd = vcol[:, DB + (TAPS + 2) * EB:NV]
        ident = sb("ident", [P, P])
        ident16 = sb("ident16", [P, P], f16)
        ones = sb("ones", [P, P])
        keep = sb("keep", [P, NCH], i32)
        eps_c = sb("eps_c", [P, TB])
        mhalf_c = sb("mhalf_c", [P, TB])
        scale_c = sb("scale_c", [P, TB])
        asum = sb("asum", [P, 3, 4])
        asum1 = sb("asum1", [P, 3])
        wscale = sb("wscale", [P, 3])
        thr = sb("thr", [P, 2, 3])
        tanh_sc = sb("tanh_sc", [P, 1])
        prod_sc = sb("prod_sc", [P, 2])
        down_sc = sb("down_sc", [P, 1])
        xs = sb("xs", [P, XSLOTS, TB, D])
        carry = sb("carry", [P, STEPS * HE])
        hist = sb("hist", [P, 2, HE, TAPS - 1])
        st = sb("st", [P, TB, 6])
        mv = sb("mv", [P, TB, 2])
        rt = sb("rt", [P, 6, TB])

        early = ExitStack()
        with early:
            wraw = [sb(f"wraw{m}", [P, F * D // P], f32, early) for m in range(3)]
            qh = w_out[:, :, :].rearrange("p e d -> p (e d)").bitcast(f16).rearrange("p (r n) -> p r n", r=2)

        xn_cin = sb("xn_cin", [P, HE * (TAPS - 1 + CH)])
        xn = xn_cin[:, 0:TB * D].rearrange("p (t d) -> p t d", t=TB)
        cin = xn_cin[:, :].rearrange("p (e t) -> p e t", e=HE)
        xh = sb("xh", [P, DB, CH], f16)
        xl = sb("xl", [P, DB, CH], f16)
        act = sb("act", [P, 2, 2 * CH])
        hh = sb("hh", [P, FB, CH], f16)
        hl = sb("hl", [P, FB, CH], f16)
        xrT = sb("xrT", [P, DB, CH])
        tmp = sb("tmp", [P, HE * CH])
        tmp_h = tmp[:, :].rearrange("p (e t) -> p e t", e=HE)
        xr = tmp[:, :].rearrange("p (t d) -> p t d", t=TB)
        xc = sb("xc", [P, EB, CH])
        xw = sb("xw", [P, HE, CH])
        gz = sb("gz", [P, EB, CH])
        d1 = sb("d1", [P, CH])
        bcn = sb("bcn", [P, TB, 2 * N])
        bT = sb("bT", [N, CH])
        ccur = sb("ccur", [P, TB, N])
        delta = sb("delta", [P, EB, CH])
        u = sb("u", [P, HE, CH])
        bb = sb("bb", [P, 2, PLANES, CH])
        abar = sb("abar", [P, RING, HE, 1 + CH])
        h = sb("h", [P, RING, HE, 1 + CH])
        y = sb("y", [P, TB, HE * P])

        ps = ctx.enter_context(nc.psum_tensor("ps", [P, 8, 512], f32))
        hT = ps[:, 0:2, :]
        pair = [ps[:, 2 + 2 * p:4 + 2 * p, :] for p in range(NPAIR)]

        x_loaded, out_stored = sem("x_loaded"), sem("out_stored")
        raw_loaded = [[sem(f"raw{m}_loaded{q}") for q in range(QUARTERS)] for m in range(3)]
        vec_loaded, alog_loaded = sem("vec_loaded"), sem("alog_loaded")
        win_loaded, wsk_loaded, wout_loaded = sem("win_loaded"), sem("wsk_loaded"), sem("wout_loaded")
        wd1_loaded, wd2_loaded, wbc_loaded = sem("wd1_loaded"), sem("wd2_loaded"), sem("wbc_loaded")
        abar_zero = sem("abar_zero")
        const_zero, const_ready, dve_const = sem("const_zero"), sem("const_ready"), sem("dve_const")
        abs_ready, asum_ready, asums_ready = sem("abs_ready"), sem("asum_ready"), sem("asums_ready")
        scale_step, gt_ready, q_ready = sem("scale_step"), sem("gt_ready"), sem("q_ready")
        qt_ready, q_saved = sem("qt_ready"), sem("q_saved")
        vec_ready, vcol_ready, vec_step = sem("vec_ready"), sem("vcol_ready"), sem("vec_step")
        a_exp, a_done = sem("a_exp"), sem("a_done")
        pair_ready = [sem(f"pair_ready{p}") for p in range(NPAIR)]
        pair_used = [sem(f"pair_used{p}") for p in range(NPAIR)]
        ub_ready, abar_ready = sem("ub_ready"), sem("abar_ready")
        b_stored = sem("b_stored")
        bb_loaded = [sem("bb_loaded0"), sem("bb_loaded1")]
        scanned, hT_ready = sem("scanned"), sem("hT_ready")
        y_added = [sem("y_added0"), sem("y_added1")]
        carry_saved, c_copied = sem("carry_saved"), sem("c_copied")
        ln_stats, ln_moments, xn_ready = sem("ln_stats"), sem("ln_moments"), sem("xn_ready")
        rstd_step, rms_step = sem("rstd_step"), sem("rms_step")
        xr_ready, x12_ready = sem("xr_ready"), sem("x12_ready")
        xh_ready, tanh_ready, silu_ready = sem("xh_ready"), sem("tanh_ready"), sem("silu_ready")
        hh_ready, hl_ready = sem("hh_ready"), sem("hl_ready")
        hist_step, conv_step = sem("hist_step"), sem("conv_step")
        ctanh_ready, xc_ready, xw_ready = sem("ctanh_ready"), sem("xc_ready"), sem("xw_ready")
        sp_step, delta_ready, u_ready = sem("sp_step"), sem("delta_ready"), sem("u_ready")
        gtanh_ready, z_ready = sem("gtanh_ready"), sem("z_ready")
        pool_go, dve_go = sem("pool_go"), sem("dve_go")
        pe_go, sp_go = sem("pe_go"), sem("sp_go")

        free = [p for p in range(NPAIR) if p != PAIR_OF["fill"]["T1"]]
        q_banks = [hT[:, 0, :], hT[:, 1, :], pair[free[0]][:, 0, :], pair[free[0]][:, 1, :]]
        sums = pair[free[1]][:, 0, :]
        vecs = pair[free[1]][:, 1, :]
        QB = len(q_banks)
        UPGATE_SAVED = 4 * QB
        ALL_SAVED = UPGATE_SAVED + 2 * QUARTERS
        HALF_COLS = F * D // P // 2
        DOWN_SLOT = [SLOT_OF["fill"][f"UG1_{r}"] for r in range(QUARTERS)]

        block = ctx.enter_context(nc.Block())

        def phases(eng, run):
            run("fill", -1)
            run("first", 0)
            with eng.Fori(1, NCH - 1) as i:
                run("loop", i)
            run("last", NCH - 1)
            run("drain", NCH)

        def hidden_units(ph, s):
            return [(int(n[2]), int(n[4])) for n in ORDER[ph] if n[:2] == "UG" and after(ph, n, 1, s)]

        @block.sync
        def _(sp):
            def load_raw(m, w):
                for q in range(QUARTERS):
                    sp.dma_start(wraw[m][:, q * F:(q + 1) * F].rearrange("p (f d) -> p f d", d=w.shape[1]),
                                 w[q * F * P // w.shape[1]:(q + 1) * F * P // w.shape[1], :].rearrange("(f p) d -> p f d", p=P)
                                 ).then_inc(raw_loaded[m][q], 16)

            load_raw(0, W_up)
            sp.dma_start(vrow[0:DB, :], norm_w.rearrange("(r p) -> r p", p=P)).then_inc(vec_loaded, 16)
            o = DB
            sp.dma_start(vrow[o:o + TAPS * EB, :], conv_w.rearrange("k o (r p) -> (k o r) p", p=P)).then_inc(vec_loaded, 16)
            o += TAPS * EB
            for v in (conv_b, b_delta_2, W_D):
                sp.dma_start(vrow[o:o + EB, :], v.rearrange("(r p) -> r p", p=P)).then_inc(vec_loaded, 16)
                o += EB
            sp.dma_start(xs[:, 0, :, :], x_dram[0]).then_inc(x_loaded, 16)
            load_raw(1, W_gate)
            load_raw(2, W_down)
            sp.dma_start(a_neg[:, :, :], A_log.rearrange("(e p) n -> p e n", p=P)).then_inc(alog_loaded, 16)
            sp.dma_start(w_in[:, :, :], W_in.rearrange("(d p) e -> p d e", p=P)).then_inc(win_loaded, 16)
            sp.dma_start(w_d1[:, :, :], W_delta_1.rearrange("(e p) r -> p e r", p=P)).then_inc(wd1_loaded, 16)
            sp.dma_start(w_bc[:, :, 0:N], W_B.rearrange("(e p) n -> p e n", p=P)).then_inc(wbc_loaded, 16)
            sp.dma_start(w_bc[:, :, N:2 * N], W_C.rearrange("(e p) n -> p e n", p=P)).then_inc(wbc_loaded, 16)
            sp.dma_start(w_d2[:, :], W_delta_2).then_inc(wd2_loaded, 16)
            sp.dma_start(w_skip[:, :, :], W_skip.rearrange("(d p) e -> p d e", p=P)).then_inc(wsk_loaded, 16)

            def load_w_out():
                sp.wait_ge(q_saved, ALL_SAVED)
                sp.dma_start(w_out[:, :, :], W_out.rearrange("(e p) d -> p e d", p=P)).then_inc(wout_loaded, 16)

            def load_x(c):
                sp.wait_ge(x_loaded, 16 * c)
                sp.dma_start(xs[:, bass.ds(c % XSLOTS, 1), :, :].rearrange("p s t d -> p (s t) d"),
                             x_dram[bass.ds(c, 1)].rearrange("s p t d -> p (s t) d")).then_inc(x_loaded, 16)

            def store(ph, i):
                pr, before = job_no(ph, i, "DN2")
                sp.wait_ge(pair_used[pr], before + 1)
                sp.sem_inc(sp_go, 1)
                sp.dma_start(out_dram[bass.ds(i - 1, 1)].rearrange("s p t d -> p (s t) d"),
                             xs[:, bass.ds((i - 1) % XSLOTS, 1), :, :].rearrange("p s t d -> p (s t) d")
                             ).then_inc(out_stored, 16)
                sp.wait_ge(out_stored, 16 * i)
                sp.sem_inc(sp_go, 1)

            def store_b(ph, i):
                c = i + 1
                pr, before = job_no(ph, i, "BT")
                sp.wait_ge(pair_used[pr], before + 1)
                sp.sem_inc(sp_go, 1)
                if not isinstance(c, int) or c:
                    sp.wait_ge(bb_loaded[1], 16 * planes_loaded(c - 1, LOADS - 1))
                    sp.sem_inc(sp_go, 1)
                sp.dma_start(b_dram, bT[:, :]).then_inc(b_stored, 16)
                sp.wait_ge(b_stored, 16 * (c + 1))
                sp.sem_inc(sp_go, 1)

            def load_planes(c, q):
                if not isinstance(c, int) or c or q >= 2:
                    last = max(s for s in range(STEPS) if planes_of(s) == (q - 2) % LOADS)
                    sp.wait_ge(ub_ready, STEPS * (c - (q < 2)) + last + 1)
                    sp.sem_inc(sp_go, 1)
                g = q % (N // PLANES)
                sp.dma_start(bb[:, q % 2, :, :], b_dram[PLANES * g:PLANES * (g + 1), :].partition_broadcast(P)
                             ).then_inc(bb_loaded[q % 2], 16)

            def run(ph, i):
                if ph == "fill":
                    load_x(1)
                    load_w_out()
                if ph in ("first", "loop"):
                    if ph == "first":
                        load_x(2)
                    else:
                        sp.wait_ge(x_loaded, 16 * i + 32)
                        sp.sem_inc(sp_go, 1)
                        with_next = i + 2
                        sp.dma_start(xs[:, bass.ds(with_next % XSLOTS, 1), :, :].rearrange("p s t d -> p (s t) d"),
                                     x_dram[bass.ds(with_next % NCH, 1)].rearrange("s p t d -> p (s t) d")
                                     ).then_inc(x_loaded, 16)
                if ph in ("first", "loop", "last"):
                    for q in range(2, LOADS):
                        load_planes(i, q)
                if ph in ("fill", "first", "loop"):
                    store_b(ph, i)
                    for q in range(2):
                        load_planes(i + 1, q)
                if ph in ("loop", "last", "drain"):
                    store(ph, i)

            phases(sp, run)
            sp.wait_ge(out_stored, 16 * NCH)

        @block.gpsimd
        def _(pool):
            def go():
                pool.sem_inc(pool_go, 1)

            pl = nc.gpsimd
            pl.memset(ident[:, :], 0.0).then_inc(const_zero, 1)
            pl.memset(ident16[:, :], 0.0).then_inc(const_zero, 1)
            pl.memset(ones[:, :], 1.0)
            pl.memset(eps_c[:, :], EPS)
            pl.memset(mhalf_c[:, :], -0.5)
            pl.memset(scale_c[:, :], XN_SCALE)
            pool.wait_ge(const_zero, 2)
            pl.affine_select(out=ident[:, :], in_=ident[:, :], compare_op=ALU.not_equal, fill=1.0, base=0,
                             pattern=[[-1, P]], channel_multiplier=1).then_inc(const_ready, 1)
            pl.affine_select(out=ident16[:, :], in_=ident16[:, :], compare_op=ALU.not_equal, fill=1.0, base=0,
                             pattern=[[-1, P]], channel_multiplier=1).then_inc(const_ready, 1)
            def scan_columns():
                pool.wait_ge(a_exp, 1)
                pl.tensor_scalar(a_neg[:, :, :], a_neg[:, :, :], -1.0, None, ALU.mult).then_inc(a_done, 1)
                pool.wait_ge(q_saved, ALL_SAVED)
                go()
                pl.memset(abar[:, :, :, 0], 0.0).then_inc(abar_zero, 1)
                pool.wait_ge(dve_const, B + 3)
                pool.wait_ge(vec_step, 2)

            def u_times_b(ph, i, s):
                S, half, n = STEPS * i + s, s // N, state_of(s)
                q = planes_of(s)
                if s == 0 or q > planes_of(s - 1):
                    need(pool, bb_loaded[q % 2], 16 * planes_loaded(i, q))
                if s % N == 0:
                    u_of(i, half, S)
                    need(pool, u_ready, 2 * i + half + 1)
                used = S - ring_lag(s)
                need(pool, hT_ready, 2 * used + 2)
                if ph != "last" or s < ring_lag(s):
                    need(pool, carry_saved, used + 1)
                go()
                pl.tensor_copy(h[:, s % RING, :, 0], carry[:, HE * s:HE * (s + 1)])
                pl.tensor_tensor(h[:, s % RING, :, 1:], u[:, :, :],
                                 bb[:, planes_of(s) % 2, s % PLANES:s % PLANES + 1, :].broadcast_to([P, HE, CH]),
                                 ALU.mult).then_inc(ub_ready, 1)

            def rstd(ph, i, kind):
                r = rstd_run(ph, i, kind)
                need(pool, ln_moments, TB * ln_run(ph, i, kind) + TB)
                pl.tensor_tensor(rt[:, 0, :], mv[:, :, 1], eps_c[:, :], ALU.add).then_inc(rstd_step, 1)
                need(pool, rstd_step, 3 * r + 1)
                pl.tensor_tensor(rt[:, 1, :], rt[:, 0, :], mhalf_c[:, :], ALU.pow).then_inc(rstd_step, 1)
                need(pool, rstd_step, 3 * r + 2)
                pl.tensor_tensor(rt[:, 2, :], rt[:, 1, :], scale_c[:, :], ALU.mult).then_inc(rstd_step, 1)

            def rms(ph, i):
                k = i + 1
                need(pool, ln_moments, TB * ln_run(ph, i, "p") + TB)
                pl.tensor_tensor(rt[:, 0, :], mv[:, :, 1], eps_c[:, :], ALU.add).then_inc(rms_step, 1)
                need(pool, rms_step, 6 * k + 1)
                pl.tensor_tensor(rt[:, 1, :], rt[:, 0, :], mhalf_c[:, :], ALU.pow).then_inc(rms_step, 1)
                need(pool, rms_step, 6 * k + 2)
                pl.tensor_tensor(rt[:, 3, :], rt[:, 1, :], rt[:, 1, :], ALU.mult).then_inc(rms_step, 1)
                need(pool, rms_step, 6 * k + 3)
                pl.tensor_tensor(rt[:, 4, :], rt[:, 3, :], mv[:, :, 1], ALU.mult).then_inc(rms_step, 1)
                need(pool, rms_step, 6 * k + 4)
                pl.tensor_tensor(rt[:, 3, :], rt[:, 4, :], eps_c[:, :], ALU.add).then_inc(rms_step, 1)
                need(pool, rms_step, 6 * k + 5)
                pl.tensor_tensor(rt[:, 5, :], rt[:, 3, :], mhalf_c[:, :], ALU.pow).then_inc(rms_step, 1)

            def x12(ph, i):
                k = i + 1
                need(pool, xn_ready, TB * ln_run(ph, i, "p") + TB)
                go()
                slot = k % XSLOTS
                pl.tensor_tensor(xs[:, slot, :, :], xs[:, slot, :, :], xn[:, :, :], ALU.add).then_inc(x12_ready, 1)

            def hidden_low(ph, i, kind, p):
                g = PAIRS * ffn_run(ph, i, kind) + p
                need(pool, hh_ready, g + 1)
                pl.tensor_tensor(hl[:, 2 * p:2 * p + 2, :], act[:, p % 2, :].rearrange("q (f t) -> q f t", f=2),
                                 hh[:, 2 * p:2 * p + 2, :], ALU.subtract).then_inc(hl_ready, 1)

            def u_of(c, half, S):
                need(pool, ub_ready, S)
                need(pool, delta_ready, 2 * c + half + 1)
                need(pool, xc_ready, 2 * c + half + 1)
                go()
                pl.tensor_tensor(u[:, :, :], delta[:, half * HE:(half + 1) * HE, :],
                                 xc[:, half * HE:(half + 1) * HE, :], ALU.mult).then_inc(u_ready, 1)

            def x_times_d(i):
                need(pool, z_ready, 2 * i)
                need(pool, xc_ready, 2 * i + 2)
                go()
                pl.tensor_tensor(xw[:, :, :], xc[:, HE:, :], wd[:, HE:].unsqueeze(2).broadcast_to([P, HE, CH]),
                                 ALU.mult).then_inc(xw_ready, 1)

            def run(ph, i):
                has = PHASES[ph]
                scan = "SK_0" in has
                if ph == "first":
                    scan_columns()
                if scan:
                    for s in range(AHEAD):
                        u_times_b(ph, i, s)
                for s in range(STEPS + 2):
                    if scan and s + AHEAD < STEPS:
                        u_times_b(ph, i, s + AHEAD)
                    if after(ph, "OM", 0, s):
                        rstd(ph, i, "2")
                    for kind, p in hidden_units(ph, s):
                        hidden_low(ph, i, kind, p)
                    if after(ph, "DN1", 0, s):
                        rms(ph, i)
                    if after(ph, "DN1", 1, s):
                        x12(ph, i)
                    if s == XD_SLOT and scan:
                        x_times_d(i)
                    if s == NEXT_LN and "T1" in has:
                        rstd(ph, i, "n")

            rstd("fill", -1, "1")
            pool.wait_ge(q_saved, UPGATE_SAVED)
            phases(pool, run)

        @block.scalar
        def _(sc):
            ac = nc.scalar

            def ready(ph, i, name):
                pr, before = job_no(ph, i, name)
                need(sc, pair_ready[pr], before + 1)
                return pr, pair[pr]

            def flat(pp):
                return pp.rearrange("p a b -> p (a b)")

            def x_high(ph, i, kind):
                pr, pp = ready(ph, i, f"T{kind}")
                ac.activation(xh[:, :, :].rearrange("p d t -> p (d t)"), flat(pp), ACT.Copy).then_inc(xh_ready, 1)

            junk = q_down[:, :, :].rearrange("p f d -> p (f d)").bitcast(f32)

            def sum_abs(m, q):
                sc.wait_ge(raw_loaded[m][q], 16)
                if m or q:
                    sc.wait_ge(abs_ready, QUARTERS * m + q)
                ac.activation(junk, wraw[m][:, q * F:(q + 1) * F], ACT.Abs, accum_out=asum[:, m, q:q + 1]).then_inc(abs_ready, 1)

            def save_q(m, part):
                for b in range(QB):
                    sc.wait_ge(qt_ready, QB * (2 * m + part) + b + 1)
                    ac.activation(qT[m][:, b, part * (F // 2):(part + 1) * (F // 2)], q_banks[b].bitcast(f16), ACT.Copy,
                                  saturate=False).then_inc(q_saved, 1)

            def save_q_down(r):
                for b in range(2):
                    sc.wait_ge(qt_ready, UPGATE_SAVED + 2 * r + b + 1)
                    ac.activation(q_down[:, 8 * b:8 * b + 8, r * P:(r + 1) * P],
                                  q_banks[b].bitcast(f16).rearrange("p (f d) -> p f d", f=8), ACT.Copy,
                                  saturate=False).then_inc(q_saved, 1)

            for q in range(QUARTERS):
                sum_abs(0, q)
            for q in range(QUARTERS):
                sum_abs(1, q)
            save_q(0, 0)
            save_q(0, 1)
            for q in range(QUARTERS):
                sum_abs(2, q)
            sc.wait_ge(alog_loaded, 16)
            ac.activation(a_neg[:, :, :], a_neg[:, :, :], ACT.Exp).then_inc(a_exp, 1)
            x_high("fill", -1, 1)
            save_q(1, 0)
            save_q(1, 1)
            sc.wait_ge(vec_step, 2)
            sc.wait_ge(q_saved, UPGATE_SAVED)

            def exps(ph, i, s):
                S, half, n = STEPS * i + s, s // N, state_of(s)
                if s % N == 0:
                    need(sc, delta_ready, 2 * i + half + 1)
                need(sc, scanned, S - ring_lag(s) + 1)
                for e in range(HE):
                    k = half * HE + e
                    ins = ac.activation(abar[:, s % RING, e, 1:], delta[:, k, :], ACT.Exp, scale=a_neg[:, k, n:n + 1])
                ins.then_inc(abar_ready, 1)

            def tanh_up(ph, i, kind, p):
                g = PAIRS * ffn_run(ph, i, kind) + p
                need(sc, hl_ready, g - 1)
                pr, pp = ready(ph, i, f"UG{kind}_{p}")
                ac.activation(act[:, p % 2, :], pp[:, 0, :], ACT.Tanh, scale=tanh_sc[:, 0:1]).then_inc(tanh_ready, 1)

            def hidden_high(ph, i, kind, p):
                pr, before = job_no(ph, i, f"UG{kind}_{p}")
                need(sc, pair_used[pr], before + 1)
                ac.activation(hh[:, 2 * p:2 * p + 2, :], act[:, p % 2, :].rearrange("q (f t) -> q f t", f=2),
                              ACT.Copy).then_inc(hh_ready, 1)

            def x_norm_T(ph, i):
                pr, pp = ready(ph, i, "Tp")
                for d in range(DB):
                    ins = ac.activation(xrT[:, d, :], flat(pp)[:, d * CH:(d + 1) * CH], ACT.Copy, scale=nw[:, d:d + 1])
                ins.then_inc(pair_used[pr], 1)

            def conv_in(ph, i, half):
                need(sc, conv_step, CONV_STEPS * (2 * (i + 1) + half))
                need(sc, x12_ready, i + 2)
                pr, pp = ready(ph, i, f"IN_{half}")
                ac.activation(cin[:, :, TAPS - 1:], flat(pp).rearrange("p (e t) -> p e t", e=HE), ACT.Copy)
                if half == 0:
                    need(sc, z_ready, 2 * i + 1)
                else:
                    need(sc, xw_ready, i + 1)
                for e in range(HE):
                    b = half * HE + e
                    w = cw[:, (TAPS - 1) * EB + b:(TAPS - 1) * EB + b + 1]
                    ins = ac.activation(xc[:, b, :], flat(pp)[:, e * CH:(e + 1) * CH], ACT.Identity, scale=w, bias=cb[:, b:b + 1])
                ins.then_inc(pair_used[pr], 1)

            def conv_tanh(i, half):
                c = i + 1
                need(sc, conv_step, CONV_STEPS * (2 * c + half + 1))
                need(sc, xc_ready, 2 * c + half)
                ac.activation(tmp_h, xc[:, half * HE:(half + 1) * HE, :], ACT.Tanh).then_inc(ctanh_ready, 1)

            def delta_rank(ph, i):
                pr, pp = ready(ph, i, "D1")
                ac.activation(d1[:, :], pp[:, 0, 0:CH], ACT.Copy).then_inc(pair_used[pr], 1)

            def b_and_c(ph, i):
                need(sc, c_copied, i + 1)
                pr, pp = ready(ph, i, "BC")
                ac.activation(bcn[:, :, :], pp[:, 0, 0:TB * 2 * N].rearrange("p (t n) -> p t n", t=TB),
                              ACT.Copy).then_inc(pair_used[pr], 1)

            def softplus_in(ph, i, half):
                pr, pp = ready(ph, i, f"D2_{half}")
                for e in range(HE):
                    b = half * HE + e
                    ins = ac.activation(delta[:, b, :], flat(pp)[:, e * CH:(e + 1) * CH], ACT.Identity, bias=b2[:, b:b + 1])
                ins.then_inc(pair_used[pr], 1)

            def softplus_log(ph, i, half):
                c = i + 1 if half == 0 else i
                pr, before = job_no(ph, i, f"D2_{half}")
                need(sc, pair_used[pr], before + 1)
                v = delta[:, half * HE:(half + 1) * HE, :]
                ac.activation(tmp_h, v, ACT.Abs).then_inc(sp_step, 1)
                need(sc, sp_step, 3 * (2 * c + half) + 1)
                ac.activation(tmp_h, tmp_h, ACT.Exp, scale=-1.0).then_inc(sp_step, 1)
                need(sc, sp_step, 3 * (2 * c + half) + 2)
                ac.activation(tmp_h, tmp_h, ACT.Ln, bias=1.0).then_inc(sp_step, 1)

            def b_rows(ph, i):
                need(sc, b_stored, 16 * (i + 1))
                pr, pp = ready(ph, i, "BT")
                ac.activation(bT[:, :], pp[0:N, 0, 0:CH], ACT.Copy).then_inc(pair_used[pr], 1)

            def skip_tanh(ph, i, half):
                pr, pp = ready(ph, i, f"SK_{half}")
                ac.activation(gz[:, half * HE:(half + 1) * HE, :].rearrange("p e t -> p (e t)"), flat(pp), ACT.Tanh,
                              scale=0.5).then_inc(gtanh_ready, 1)

            def run(ph, i):
                has = PHASES[ph]
                scan = "SK_0" in has

                def evacuate(name):
                    if name[:2] == "UG":
                        tanh_up(ph, i, int(name[2]), int(name[4]))
                    elif name in ("T1", "T2"):
                        x_high(ph, i, int(name[1]))
                    elif name == "Tp":
                        x_norm_T(ph, i)
                    elif name[:2] == "IN":
                        conv_in(ph, i, int(name[3]))
                    elif name == "D1":
                        delta_rank(ph, i)
                    elif name == "BC":
                        b_and_c(ph, i)
                    elif name[:2] == "SK":
                        skip_tanh(ph, i, int(name[3]))
                    elif name == "BT":
                        b_rows(ph, i)
                    elif name[:2] == "D2":
                        softplus_in(ph, i, int(name[3]))

                if ph == "first":
                    sc.wait_ge(a_done, 1)
                    sc.wait_ge(abar_zero, 1)
                if scan:
                    for s in range(AHEAD):
                        exps(ph, i, s)
                for s in range(STEPS + 3):
                    if scan and s + AHEAD < STEPS:
                        exps(ph, i, s + AHEAD)
                    for name in results(ph, s, late=False):
                        evacuate(name)
                    for kind, p in hidden_units(ph, s):
                        hidden_high(ph, i, kind, p)
                    for half in range(2):
                        if after(ph, f"D2_{half}", 1, s):
                            softplus_log(ph, i, half)
                        if after(ph, f"IN_{half}", 2, s):
                            conv_tanh(i, half)
                    for name in results(ph, s, late=True):
                        evacuate(name)
                    if ph == "fill" and s - 1 in DOWN_SLOT:
                        save_q_down(DOWN_SLOT.index(s - 1))
                        if s - 1 == DOWN_SLOT[-1]:
                            sc.wait_ge(q_saved, ALL_SAVED)

            phases(sc, run)

        @block.vector
        def _(ve):
            v = nc.vector

            def go():
                ve.sem_inc(dve_go, 1)

            v.memset(keep[:, :], -1).then_inc(dve_const, 1)
            ve.wait_ge(dve_const, 1)
            for b in range(B):
                v.memset(keep[:, b * CPB:b * CPB + 1], 0).then_inc(dve_const, 1)
            v.memset(carry[:, :], 0.0).then_inc(dve_const, 1)
            v.memset(hist[:, :, :, :], 0.0).then_inc(dve_const, 1)
            ve.wait_ge(dve_const, B + 3)

            def moments(ph, i, kind, slot):
                l = ln_run(ph, i, kind)
                go()
                for t in range(TB):
                    v.bn_stats(st[:, t, :], xs[:, slot, t, :]).then_inc(ln_stats, 1)
                need(ve, ln_stats, TB * l + TB)
                go()
                for t in range(TB):
                    v.bn_aggr(mv[:, t, :], st[:, t, :]).then_inc(ln_moments, 1)

            def normalise(ph, i, kind, slot):
                row = 2
                if kind == "p":
                    row = 1
                    need(ve, rms_step, 6 * (i + 1) + 6)
                else:
                    need(ve, rstd_step, 3 * rstd_run(ph, i, kind) + 3)
                l = ln_run(ph, i, kind)
                for t in range(TB):
                    v.tensor_scalar(xn[:, t, :], xs[:, slot, t, :], mv[:, t, 0:1], rt[:, row, t:t + 1], ALU.subtract,
                                    ALU.mult).then_inc(xn_ready, 1)

            def ready(ph, i, name):
                pr, before = job_no(ph, i, name)
                need(ve, pair_ready[pr], before + 1)
                return pr, pair[pr]

            def flat(pp):
                return pp.rearrange("p a b -> p (a b)")

            def x_low(ph, i, kind):
                need(ve, xh_ready, ffn_run(ph, i, kind) + 1)
                pr, pp = ready(ph, i, f"T{kind}")
                v.tensor_tensor(xl[:, :, :].rearrange("p d t -> p (d t)"), flat(pp), xh[:, :, :].rearrange("p d t -> p (d t)"),
                                ALU.subtract).then_inc(pair_used[pr], 1)

            def scale(m):
                ve.wait_ge(abs_ready, QUARTERS * (m + 1))
                v.reduce_sum(asum1[:, m:m + 1], asum[:, m, :], AX.X).then_inc(asum_ready, 1)
                ve.wait_ge(asums_ready, m + 1)
                v.tensor_scalar(wscale[:, m:m + 1], sums[:, m:m + 1], 1.0 / (F * D), TEPS, ALU.mult,
                                ALU.add).then_inc(scale_step, 1)
                ve.wait_ge(scale_step, 3 * m + 1)
                v.tensor_scalar(thr[:, 0, m:m + 1], wscale[:, m:m + 1], 0.5, None, ALU.mult).then_inc(scale_step, 1)
                v.tensor_scalar(thr[:, 1, m:m + 1], wscale[:, m:m + 1], -0.5, None, ALU.mult).then_inc(scale_step, 1)
                ve.wait_ge(scale_step, 3 * m + 3)

            def ternary(m, piece, lo, cols):
                if piece >= 2:
                    ve.wait_ge(qt_ready, QB * (piece - 1) if piece <= 5 else UPGATE_SAVED + 2 * (piece - 5))
                src, dst = wraw[m][:, lo:lo + cols], qh[:, piece % 2, 0:cols]
                v.tensor_scalar(dst, src, thr[:, 0, m:m + 1], None, ALU.is_gt).then_inc(gt_ready, 1)
                ve.wait_ge(gt_ready, piece + 1)
                v.scalar_tensor_tensor(out=dst, in0=src, scalar=thr[:, 1, m:m + 1], in1=dst, op0=ALU.is_lt,
                                       op1=ALU.subtract).then_inc(q_ready, 1)

            scale(0)
            for part in range(2):
                ternary(0, part, part * HALF_COLS, HALF_COLS)
            scale(1)
            ternary(1, 2, 0, HALF_COLS)
            ve.wait_ge(x_loaded, 16)
            moments("fill", -1, "1", 0)
            ve.wait_ge(vec_ready, 1)
            v.tensor_copy(vcol[:, :], vecs[:, 0:NV]).then_inc(vcol_ready, 1)
            ve.wait_ge(vcol_ready, 1)
            v.tensor_scalar(vcol[:, DB:DB + (TAPS + 1) * EB], vcol[:, DB:DB + (TAPS + 1) * EB], 0.5, None,
                            ALU.mult).then_inc(vec_step, 1)
            normalise("fill", -1, "1", 0)
            ternary(1, 3, HALF_COLS, HALF_COLS)
            x_low("fill", -1, 1)
            scale(2)
            v.tensor_scalar(tanh_sc[:, :], wscale[:, 0:1], -0.5 / XN_SCALE, None, ALU.mult).then_inc(vec_step, 1)
            v.tensor_tensor(prod_sc[:, 0:1], wscale[:, 0:1], wscale[:, 1:2], ALU.mult).then_inc(scale_step, 1)
            ve.wait_ge(scale_step, 10)
            v.tensor_tensor(prod_sc[:, 1:2], prod_sc[:, 0:1], wscale[:, 2:3], ALU.mult).then_inc(scale_step, 1)
            ve.wait_ge(scale_step, 11)
            v.tensor_scalar(down_sc[:, :], prod_sc[:, 1:2], -0.5 * 0.5 / (HID_SCALE * XN_SCALE * XN_SCALE), None,
                            ALU.mult).then_inc(scale_step, 1)
            ve.wait_ge(scale_step, 12)

            def start_chunk(i):
                need(ve, delta_ready, 2 * i + 1)
                for t in range(TB):
                    need(ve, y_added[t], STEPS * i)
                go()
                v.tensor_copy(ccur[:, :, :], bcn[:, :, N:2 * N]).then_inc(c_copied, 1)

            def scan_of(i, s):
                S = STEPS * i + s
                need(ve, abar_ready, S + 1)
                need(ve, ub_ready, S + 1)
                hh_s = h[:, s % RING, :, :].rearrange("p e t -> p (e t)")
                v.tensor_tensor_scan(hh_s, abar[:, s % RING, :, :].rearrange("p e t -> p (e t)"), hh_s, 0.0, ALU.mult,
                                     ALU.add).then_inc(scanned, 1)

            def save_carry(i, s):
                need(ve, scanned, STEPS * i + s + 1)
                nxt = keep[:, i + 1:i + 2] if isinstance(i, int) else keep[:, bass.ds(i + 1, 1)]
                v.tensor_tensor(carry[:, HE * s:HE * (s + 1)].bitcast(i32), h[:, s % RING, :, CH].bitcast(i32),
                                nxt.broadcast_to([P, HE]), ALU.bitwise_and).then_inc(carry_saved, 1)

            def y_add(ph, i, s):
                S, half, n = STEPS * i + s, s // N, state_of(s)
                if s == 0:
                    need(ve, c_copied, i + 1)
                if s % N == 0 and (half == 1 or ph == "loop" or ph == "last"):
                    pr, before = job_no(ph, i, f"YT_{1 - half}")
                    need(ve, pair_ready[pr], before + 1)
                for t in range(TB):
                    need(ve, hT_ready, 2 * S + t + 1)
                    yy = y[:, t, :]
                    cc = ccur[:, t, n:n + 1]
                    if s % N == 0:
                        ins = v.tensor_scalar(yy, hT[:, t, :], cc, None, ALU.mult)
                    else:
                        need(ve, y_added[t], S)
                        ins = v.scalar_tensor_tensor(out=yy, in0=hT[:, t, :], scalar=cc, in1=yy, op0=ALU.mult, op1=ALU.add)
                    ins.then_inc(y_added[t], 1)

            def rms_scaled(ph, i):
                need(ve, xn_ready, TB * ln_run(ph, i, "p") + TB)
                for t in range(TB):
                    ins = v.tensor_scalar(xr[:, t, :], xn[:, t, :], rt[:, 5, t:t + 1], None, ALU.mult)
                ins.then_inc(xr_ready, 1)

            def hidden(ph, i, kind, p):
                g = PAIRS * ffn_run(ph, i, kind) + p
                need(ve, tanh_ready, g + 1)
                pr, pp = ready(ph, i, f"UG{kind}_{p}")
                a = act[:, p % 2, :]
                v.scalar_tensor_tensor(out=a, in0=a, scalar=1.0, in1=pp[:, 0, :], op0=ALU.add, op1=ALU.mult).then_inc(silu_ready, 1)
                need(ve, silu_ready, g + 1)
                v.scalar_tensor_tensor(out=a, in0=pp[:, 1, :], scalar=HID_SCALE, in1=a, op0=ALU.mult,
                                       op1=ALU.mult).then_inc(pair_used[pr], 1)

            def add_to_stream(ph, i, name, slot, factor):
                pr, pp = ready(ph, i, name)
                for t in range(TB):
                    xx = xs[:, slot, t, :]
                    ins = v.scalar_tensor_tensor(out=xx, in0=pp[:, t, :], scalar=factor, in1=xx, op0=ALU.mult, op1=ALU.add)
                ins.then_inc(pair_used[pr], 1)
                need(ve, pair_used[pr], job_no(ph, i, name)[1] + 1)

            def conv(ph, i, half, part):
                c = i + 1
                g = CONV_STEPS * (2 * c + half)
                pr, before = job_no(ph, i, f"IN_{half}")
                if part == 0:
                    need(ve, conv_step, g)
                    need(ve, x12_ready, c + 1)
                    pt, tb = job_no(ph, i, "Tp")
                    need(ve, pair_ready[pt], tb + 1)
                    v.tensor_tensor(cin[:, :, 0:TAPS - 1].bitcast(i32), hist[:, half, :, :].bitcast(i32),
                                    (keep[:, c:c + 1] if isinstance(c, int) else keep[:, bass.ds(c, 1)])
                                    .unsqueeze(2).broadcast_to([P, HE, TAPS - 1]), ALU.bitwise_and).then_inc(conv_step, 1)
                    need(ve, pair_used[pr], before + 1)
                    need(ve, conv_step, g + 1)
                    v.tensor_copy(hist[:, half, :, :], cin[:, :, CH:CH + TAPS - 1]).then_inc(conv_step, 1)
                g += 2 + part * (TAPS - 1) * HE // 2
                for tap in range(TAPS - 1):
                    for e in range(HE // 2):
                        b = half * HE + part * HE // 2 + e
                        if tap:
                            need(ve, conv_step, g + HE // 2 * (tap - 1) + e + 1)
                        v.scalar_tensor_tensor(out=xc[:, b, :], in0=cin[:, part * HE // 2 + e, tap:tap + CH],
                                               scalar=cw[:, tap * EB + b:tap * EB + b + 1], in1=xc[:, b, :], op0=ALU.mult,
                                               op1=ALU.add).then_inc(conv_step, 1)

            def conv_silu(i, half):
                c = i + 1
                need(ve, ctanh_ready, 2 * c + half + 1)
                xx = xc[:, half * HE:(half + 1) * HE, :]
                v.scalar_tensor_tensor(out=xx, in0=tmp_h, scalar=1.0, in1=xx, op0=ALU.add, op1=ALU.mult).then_inc(xc_ready, 1)

            def softplus(c, half):
                need(ve, sp_step, 3 * (2 * c + half) + 3)
                dd = delta[:, half * HE:(half + 1) * HE, :]
                v.scalar_tensor_tensor(out=dd, in0=dd, scalar=0.0, in1=tmp_h, op0=ALU.max, op1=ALU.add).then_inc(delta_ready, 1)

            def skip_gate(ph, i, half):
                need(ve, gtanh_ready, 2 * i + half + 1)
                pr, pp = ready(ph, i, f"SK_{half}")
                gg = gz[:, half * HE:(half + 1) * HE, :].rearrange("p e t -> p (e t)")
                v.scalar_tensor_tensor(out=gg, in0=gg, scalar=1.0, in1=flat(pp), op0=ALU.add, op1=ALU.mult).then_inc(pair_used[pr], 1)

            def gated(ph, i, half):
                c = i if half == 0 else i - 1
                pr, pp = ready(ph, i, f"YT_{half}")
                hb = slice(half * HE, (half + 1) * HE)
                if half == 0:
                    yx = xc[:, hb, :]
                    for e in range(HE):
                        ins = v.scalar_tensor_tensor(out=yx[:, e, :], in0=yx[:, e, :], scalar=wd[:, e:e + 1],
                                                     in1=flat(pp)[:, e * CH:(e + 1) * CH], op0=ALU.mult, op1=ALU.add)
                else:
                    need(ve, xw_ready, i)
                    yx = xw[:, :, :]
                    ins = v.tensor_tensor(yx.rearrange("p e t -> p (e t)"), flat(pp), yx.rearrange("p e t -> p (e t)"), ALU.add)
                ins.then_inc(pair_used[pr], 1)
                need(ve, pair_used[pr], job_no(ph, i, f"YT_{half}")[1] + 1)
                v.tensor_tensor(gz[:, hb, :], yx, gz[:, hb, :], ALU.mult).then_inc(z_ready, 1)

            def run(ph, i):
                scan = "SK_0" in PHASES[ph]
                if scan:
                    start_chunk(i)
                    scan_of(i, 0)
                for s in range(STEPS + 3):
                    if scan and s + 1 < STEPS:
                        scan_of(i, s + 1)
                    if scan and s < STEPS and ph != "last":
                        save_carry(i, s)
                    for name in results(ph, s, late=False):
                        use(ph, i, name)
                    if scan and 1 <= s <= STEPS:
                        y_add(ph, i, s - 1)
                    background(ph, i, s)
                    if ph == "fill" and s in DOWN_SLOT:
                        r = DOWN_SLOT.index(s)
                        ternary(2, 4 + r, r * F, F)
                    for name in results(ph, s, late=True):
                        use(ph, i, name)

            def use(ph, i, name):
                nslot = (i + 1) % XSLOTS
                pslot = (i - 1) % XSLOTS
                if name[:2] == "UG":
                    hidden(ph, i, int(name[2]), int(name[4]))
                elif name in ("T1", "T2"):
                    x_low(ph, i, int(name[1]))
                elif name == "OM":
                    add_to_stream(ph, i, "OM", pslot, 0.5)
                    moments(ph, i, "2", pslot)
                elif name == "DN1":
                    add_to_stream(ph, i, "DN1", nslot, down_sc[:, 0:1])
                    moments(ph, i, "p", nslot)
                elif name == "DN2":
                    add_to_stream(ph, i, "DN2", pslot, down_sc[:, 0:1])
                elif name[:2] == "SK":
                    skip_gate(ph, i, int(name[3]))
                elif name[:2] == "YT":
                    gated(ph, i, int(name[3]))

            def background(ph, i, s):
                has = PHASES[ph]
                nslot = (i + 1) % XSLOTS
                pslot = (i - 1) % XSLOTS

                for half in range(2):
                    if after(ph, f"IN_{half}", 0, s):
                        conv(ph, i, half, 0)
                    if after(ph, f"IN_{half}", 1, s):
                        conv(ph, i, half, 1)
                    if after(ph, f"IN_{half}", 2, s):
                        conv_silu(i, half)
                    if after(ph, f"D2_{half}", 2, s):
                        softplus(i + 1 if half == 0 else i, half)
                if after(ph, "OM", 1, s):
                    if "Tp" in has:
                        need(ve, x12_ready, i + 1)
                    normalise(ph, i, "2", pslot)
                if after(ph, "DN1", 1, s):
                    if "T2" in has:
                        pr, before = job_no(ph, i, "T2")
                        need(ve, pair_ready[pr], before + 1)
                    normalise(ph, i, "p", nslot)
                    rms_scaled(ph, i)
                if "T1" in has and s == NEXT_LN:
                    need(ve, x_loaded, 16 * (i + 3))
                    moments(ph, i, "n", (i + 2) % XSLOTS)
                if "T1" in has and s == NEXT_LN + 1:
                    need(ve, conv_step, CONV_STEPS * (2 * i + 4))
                    normalise(ph, i, "n", (i + 2) % XSLOTS)

            phases(ve, run)

        @block.tensor
        def _(pe):
            te = nc.tensor

            def sum_all(m):
                pe.wait_ge(asum_ready, m + 1)
                te.matmul(sums[:, m:m + 1], ones[:, :], asum1[:, m:m + 1], start=True, stop=True).then_inc(asums_ready, 1)

            def ternary_T(m, part):
                piece = 2 * m + part
                pe.wait_ge(q_ready, piece + 1)
                for b in range(QB):
                    if piece:
                        pe.wait_ge(q_saved, QB * (piece - 1) + b + 1)
                    for j in range(8):
                        ins = te.transpose(q_banks[b].bitcast(f16)[:, j * P:(j + 1) * P],
                                           qh[:, piece % 2, j * D + b * P:j * D + (b + 1) * P], ident16[:, :])
                    ins.then_inc(qt_ready, 1)

            def ternary_down_T(r):
                pe.wait_ge(q_ready, 4 + r + 1)
                for b in range(2):
                    if r:
                        pe.wait_ge(q_saved, UPGATE_SAVED + 2 * (r - 1) + b + 1)
                    for j in range(8):
                        f = 8 * b + j
                        ins = te.transpose(q_banks[b].bitcast(f16)[:, j * P:(j + 1) * P],
                                           qh[:, r % 2, f * P:(f + 1) * P], ident16[:, :])
                    ins.then_inc(qt_ready, 1)

            def states_T(i, s):
                S = STEPS * i + s
                need(pe, scanned, S + 1)
                for t in range(TB):
                    need(pe, y_added[t], S)
                    for e in range(HE):
                        ins = te.transpose(hT[:, t, e * P:(e + 1) * P], h[:, s % RING, e, 1 + t * P:1 + (t + 1) * P], ident[:, :])
                    ins.then_inc(hT_ready, 1)

            def opened(ph, i, name, lo=0):
                pr, before = job_no(ph, i, name)
                if lo == 0:
                    need(pe, pair_used[pr], before)
                return pr, pair[pr]

            def flat(pp):
                return pp.rearrange("p a b -> p (a b)")

            def used(ph, i, name, by):
                pr, before = job_no(ph, i, name)
                if PAIR_OF[ph][by] != pr:
                    need(pe, pair_used[pr], before + 1)

            def rows_T(ph, i, name, src):
                pr, pp = opened(ph, i, name)
                for d in range(DB):
                    for t in range(TB):
                        ins = te.transpose(flat(pp)[:, d * CH + t * P:d * CH + (t + 1) * P], src[:, t, d * P:(d + 1) * P],
                                           ident[:, :])
                ins.then_inc(pair_ready[pr], 1)

            def up_gate(ph, i, kind, p):
                name = f"UG{kind}_{p}"
                pr, pp = opened(ph, i, name)
                if p == 0:
                    used(ph, i, f"T{kind}", name)
                pe.sem_inc(pe_go, 1)
                for b, w in enumerate((q_up, q_gate)):
                    for f in range(2):
                        col = (2 * p + f) * P
                        for d in range(DB):
                            for part in (xh, xl):
                                ins = te.matmul(pp[:, b, f * CH:(f + 1) * CH], w[:, d, col:col + P], part[:, d, :],
                                                start=(d == 0 and part is xh), stop=(d == DB - 1 and part is xl))
                ins.then_inc(pair_ready[pr], 1)

            def down(ph, i, kind, lo, hi):
                name = f"DN{kind}"
                pr, pp = opened(ph, i, name, lo)
                need(pe, hl_ready, PAIRS * ffn_run(ph, i, kind) + (hi + 1) // 2)
                pe.sem_inc(pe_go, 1)
                for t in range(TB):
                    for f in range(lo, hi):
                        for part in (hh, hl):
                            ins = te.matmul(pp[:, t, :], part[:, f, t * P:(t + 1) * P], q_down[:, f, :],
                                            start=(f == 0 and part is hh), stop=(f == FB - 1 and part is hl))
                if hi == FB:
                    ins.then_inc(pair_ready[pr], 1)

            def project(ph, i, name, w, lo, hi):
                half = int(name[3])
                pr, pp = opened(ph, i, name, lo)
                for e in range(lo, hi):
                    col = (half * HE + e) * P
                    for d in range(DB):
                        ins = te.matmul(flat(pp)[:, e * CH:(e + 1) * CH], w[:, d, col:col + P], xrT[:, d, :],
                                        start=(d == 0), stop=(d == DB - 1))
                if hi == HE:
                    ins.then_inc(pair_ready[pr], 1)

            def delta_1(ph, i):
                need(pe, xc_ready, 2 * (i + 1) + 2)
                pr, pp = opened(ph, i, "D1")
                for e in range(EB):
                    ins = te.matmul(pp[:, 0, 0:CH], w_d1[:, e, :], xc[:, e, :], start=(e == 0), stop=(e == EB - 1))
                ins.then_inc(pair_ready[pr], 1)

            def b_and_c(ph, i):
                pr, pp = opened(ph, i, "BC")
                for t in range(TB):
                    for e in range(EB):
                        ins = te.matmul(pp[:, 0, t * 2 * N:(t + 1) * 2 * N], xc[:, e, t * P:(t + 1) * P], w_bc[:, e, :],
                                        start=(e == 0), stop=(e == EB - 1))
                ins.then_inc(pair_ready[pr], 1)

            def delta_2(ph, i, half):
                pr, pp = opened(ph, i, f"D2_{half}")
                if half == 0:
                    used(ph, i, "D1", "D2_0")
                for e in range(HE):
                    col = (half * HE + e) * P
                    ins = te.matmul(flat(pp)[:, e * CH:(e + 1) * CH], w_d2[:, col:col + P], d1[:, :], start=True, stop=True)
                ins.then_inc(pair_ready[pr], 1)

            def b_T(ph, i):
                pr, pp = opened(ph, i, "BT")
                used(ph, i, "BC", "BT")
                for t in range(TB):
                    ins = te.transpose(pp[0:N, 0, t * P:(t + 1) * P], bcn[:, t, 0:N], ident[:, :])
                ins.then_inc(pair_ready[pr], 1)

            def y_T(ph, i, half):
                c = i if half == 0 else i - 1
                for t in range(TB):
                    need(pe, y_added[t], STEPS * c + N * (half + 1))
                pr, pp = opened(ph, i, f"YT_{half}")
                for e in range(HE):
                    for t in range(TB):
                        ins = te.transpose(flat(pp)[:, e * CH + t * P:e * CH + (t + 1) * P], y[:, t, e * P:(e + 1) * P],
                                           ident[:, :])
                ins.then_inc(pair_ready[pr], 1)

            def out_proj(ph, i, lo, hi):
                pr, pp = opened(ph, i, "OM", lo)
                if lo == 0 or hi > HE:
                    need(pe, z_ready, 2 * i - 1 if hi <= HE else 2 * i)
                for t in range(TB):
                    for e in range(lo, hi):
                        ins = te.matmul(pp[:, t, :], gz[:, e, t * P:(t + 1) * P], w_out[:, e, :],
                                        start=(e == 0), stop=(e == EB - 1))
                if hi == EB:
                    ins.then_inc(pair_ready[pr], 1)

            def job(ph, i, name, lo, hi):
                if name[:2] == "UG":
                    up_gate(ph, i, int(name[2]), int(name[4]))
                elif name[:2] == "DN":
                    down(ph, i, int(name[2]), lo, hi)
                elif name in ("T1", "T2"):
                    need(pe, xn_ready, TB * ln_run(ph, i, name[1]) + TB)
                    rows_T(ph, i, name, xn)
                elif name == "Tp":
                    need(pe, xr_ready, i + 2)
                    rows_T(ph, i, name, xr)
                elif name[:2] == "IN":
                    if lo == 0:
                        used(ph, i, "Tp", name)
                    project(ph, i, name, w_in, lo, hi)
                elif name[:2] == "SK":
                    project(ph, i, name, w_skip, lo, hi)
                elif name == "D1":
                    delta_1(ph, i)
                elif name == "BC":
                    b_and_c(ph, i)
                elif name[:2] == "D2":
                    delta_2(ph, i, int(name[3]))
                elif name == "BT":
                    b_T(ph, i)
                elif name[:2] == "YT":
                    y_T(ph, i, int(name[3]))
                else:
                    out_proj(ph, i, lo, hi)

            pe.wait_ge(const_ready, 2)
            sum_all(0)
            ternary_T(0, 0)
            sum_all(1)
            ternary_T(0, 1)
            pe.wait_ge(vec_loaded, 16 * 5)
            te.transpose(vecs[:, 0:NV], vrow[:, :], ident[0:NV, 0:NV]).then_inc(vec_ready, 1)

            job("fill", -1, "T1", 0, 1)
            ternary_T(1, 0)
            ternary_T(1, 1)
            sum_all(2)
            pe.wait_ge(q_saved, UPGATE_SAVED)
            pe.wait_ge(scale_step, 7)

            loaded_for = {"IN_0": (win_loaded, 1), "D1": (wd1_loaded, 1), "BC": (wbc_loaded, 2), "D2_0": (wd2_loaded, 1)}

            def run(ph, i):
                has = PHASES[ph]
                scan = "SK_0" in has
                if ph == "first":
                    pe.wait_ge(wsk_loaded, 16)
                    pe.wait_ge(wout_loaded, 16)
                for s in range(STEPS):
                    for name, lo, hi in SLOTS[ph][s]:
                        if ph == "fill" and name in loaded_for and lo == 0:
                            sm, n = loaded_for[name]
                            pe.wait_ge(sm, 16 * n)
                        if (ph, name) != ("fill", "T1"):
                            job(ph, i, name, lo, hi)
                    if ph == "fill" and s - 1 in DOWN_SLOT:
                        ternary_down_T(DOWN_SLOT.index(s - 1))
                    if scan:
                        states_T(i, s)

            phases(pe, run)


_ORDER = ['resid', 'norm_w', 'W_skip', 'W_in', 'conv_w', 'conv_b', 'W_delta_1', 'W_delta_2', 'b_delta_2', 'W_B', 'W_C',
          'A_log', 'W_D', 'W_out']
_INS = [f'L0_attn_{n}' for n in _ORDER] + ['L0_ffn_W_up', 'L0_ffn_W_gate', 'L0_ffn_W_down']


def kernel(**inputs):
    import numpy as _np
    import concourse.bacc as _bacc
    from concourse import mybir as _mybir
    from concourse.bass_utils import run_bass_kernel_spmd as _run

    nc = _bacc.Bacc("TRN2", target_bir_lowering=False, num_devices=1)
    arrays, args = {}, []
    for name in _INS:
        a = _np.ascontiguousarray(inputs[name])
        arrays[f"in_{name}_dram"] = a
        args.append(nc.dram_tensor(f"in_{name}_dram", a.shape, _mybir.dt.from_np(a.dtype), kind="ExternalInput").ap())
    o = nc.dram_tensor("out_dram", (B, L, D), _mybir.dt.float32, kind="ExternalOutput").ap()
    b_scratch = nc.dram_tensor("b_scratch", (N, CH), _mybir.dt.float32, kind="Internal").ap()
    macaron_kernel(nc, *args, o, b_scratch)
    r = _run(nc, [arrays], core_ids=[0])
    return r.results[0]["out_dram"]
```
